# Optimizing a Trainium2 kernel written in Bass

```python
import numpy as np
import jax
import jax.numpy as jnp

def _softmax(x, axis=-1):
    return jax.nn.softmax(x, axis=axis)

def _gelu(x):
    return jax.nn.gelu(x, approximate=True)

def _silu(x):
    return jax.nn.silu(x)

def _sigmoid(x):
    return jax.nn.sigmoid(x)

def _layernorm(x, axis=-1, eps=1e-05):
    m = jnp.mean(x, axis=axis, keepdims=True)
    v = jnp.var(x, axis=axis, keepdims=True)
    return (x - m) / jnp.sqrt(v + eps)

def _scatter_add(tgt, idx, src, axis=0):
    return tgt.at[idx].add(src)

def _segment_sum(src, seg, n):
    return jax.ops.segment_sum(src, seg, n)
kernel_name = 'mk_macaron_d1_jaxref_r8_22ae50'

def setup_inputs(seed: int=0):
    np.random.seed(seed)
    _w = jnp.asarray

    def _L0_attn_setup():
        import jax, jax.numpy as jnp
        import numpy as np
        import math
        D_MODEL, D_C, D_R, NH = (128, 128, 32, 16)
        HD = D_MODEL // NH
        B, T = (2, 256)

        def _rope_tables(T, d_R):
            inv_freq = 1.0 / 10000.0 ** (jnp.arange(0, d_R, 2, dtype=jnp.float32) / d_R)
            t = jnp.arange(T, dtype=jnp.float32)
            freqs = jnp.outer(t, inv_freq)
            return (jnp.cos(freqs), jnp.sin(freqs))

        def _rotary_apply(x, cos, sin):
            d = x.shape[-1]
            x1, x2 = (x[..., :d // 2], x[..., d // 2:])
            return jnp.concatenate([x1 * cos - x2 * sin, x2 * cos + x1 * sin], axis=-1)
        key = jax.random.key(seed)
        ks = jax.random.split(key, 8)
        s = lambda fan_in: 1.0 / math.sqrt(fan_in)
        return {'x': jax.random.normal(ks[0], (B, T, D_MODEL), jnp.float32), 'W_kv_down': jax.random.normal(ks[1], (D_MODEL, D_C), jnp.float32) * s(D_MODEL), 'W_k_up': jax.random.normal(ks[2], (D_C, D_MODEL), jnp.float32) * s(D_C), 'W_v_up': jax.random.normal(ks[3], (D_C, D_MODEL), jnp.float32) * s(D_C), 'W_q': jax.random.normal(ks[4], (D_MODEL, D_MODEL), jnp.float32) * s(D_MODEL), 'W_q_rope': jax.random.normal(ks[5], (D_MODEL, D_R), jnp.float32) * s(D_MODEL), 'W_k_rope': jax.random.normal(ks[6], (D_C, D_R), jnp.float32) * s(D_C), 'W_o': jax.random.normal(ks[7], (D_MODEL, D_MODEL), jnp.float32) * s(D_MODEL)}
    _L0_attn_in = _L0_attn_setup()

    def _L0_ffn_setup():
        import jax, jax.numpy as jnp
        import numpy as np
        DIM = 128
        DEPTH = 6
        HEADS = 16
        DIM_HEAD = 64
        WINDOW = 32
        INNER = HEADS * DIM_HEAD
        DIM_INNER = int(DIM * 4 * 2 / 3)
        QK_SCALE = 8.0

        def shift_tokens(t):
            a, s = jnp.split(t, 2, -1)
            s = jnp.pad(s, ((0, 0), (1, 0), (0, 0)))[:, :-1]
            return jnp.concatenate([a, s], -1)

        def l2norm(t):
            return t / jnp.maximum(jnp.linalg.norm(t, axis=-1, keepdims=True), 1e-12)

        def rotate_half(x):
            x1, x2 = jnp.split(x, 2, -1)
            return jnp.concatenate([-x2, x1], -1)

        def rotary_tables(n):
            half = jnp.arange(0, DIM_HEAD, 2, dtype=jnp.float32)
            inv_freq = 1.0 / 10000.0 ** (half / DIM_HEAD)
            t = jnp.arange(n, dtype=jnp.float32)
            freqs = t[:, None] * inv_freq[None, :]
            freqs = jnp.concatenate([freqs, freqs], -1)
            base_scale = (half + 0.4 * DIM_HEAD) / (1.4 * DIM_HEAD)
            power = (t - n // 2) / (WINDOW // 2)
            scale = base_scale[None, :] ** power[:, None]
            scale = jnp.concatenate([scale, scale], -1)
            return (freqs, scale)

        def local_attention(q, k, v):
            b, h, n, d = q.shape
            w = WINDOW
            nw = n // w
            bq = q.reshape(b, h, nw, w, d)
            bk = k.reshape(b, h, nw, w, d)
            bv = v.reshape(b, h, nw, w, d)

            def look(t):
                p = jnp.pad(t, ((0, 0), (0, 0), (1, 0), (0, 0), (0, 0)))
                return jnp.concatenate([p[:, :, :nw], p[:, :, 1:]], axis=3)
            bk2, bv2 = (look(bk), look(bv))
            seq = jnp.arange(n).reshape(nw, w)
            seq_p = jnp.pad(seq, ((1, 0), (0, 0)), constant_values=-1)
            jt = jnp.concatenate([seq_p[:nw], seq_p[1:]], axis=1)
            it = seq[:, :, None]
            jb = jt[:, None, :]
            mask = (it < jb) | (it > jb + w) | (jb == -1)
            sim = jnp.einsum('bhwie,bhwje->bhwij', bq, bk2) * QK_SCALE
            sim = jnp.where(mask, -jnp.finfo(sim.dtype).max, sim)
            attn = jax.nn.softmax(sim, -1)
            out = jnp.einsum('bhwij,bhwje->bhwie', attn, bv2)
            return out.reshape(b, h, n, d)

        def attn_layer(x, Wqkv, qs, ksc, Wo):
            b, n, _ = x.shape
            qkv = x @ Wqkv
            q, k, v = jnp.split(qkv, 3, -1)
            sh = lambda t: t.reshape(b, n, HEADS, DIM_HEAD).transpose(0, 2, 1, 3)
            q, k, v = (sh(q), sh(k), sh(v))
            q = l2norm(q) * qs
            k = l2norm(k) * ksc
            freqs, scale = rotary_tables(n)
            cos, sin = (jnp.cos(freqs), jnp.sin(freqs))
            q = q * cos * scale + rotate_half(q) * sin * scale
            inv = 1.0 / scale
            k = k * cos * inv + rotate_half(k) * sin * inv
            out = local_attention(q, k, v)
            out = out.transpose(0, 2, 1, 3).reshape(b, n, INNER)
            return out @ Wo

        def ffn_layer(x, g, bln, W1, b1, W2, b2):
            mu = x.mean(-1, keepdims=True)
            var = ((x - mu) ** 2).mean(-1, keepdims=True)
            xn = (x - mu) / jnp.sqrt(var + 1e-05) * g + bln
            hg = xn @ W1 + b1
            a, gate = jnp.split(hg, 2, -1)
            return a * jax.nn.gelu(gate, approximate=False) @ W2 + b2
        key = jax.random.key(seed)
        ks = jax.random.split(key, 8)
        B, N = (2, 256)
        init = lambda k, shape: jax.random.normal(k, shape, jnp.float32) * 0.02
        return {'x': jax.random.normal(ks[0], (B, N, DIM), jnp.float32), 'Wqkv': init(ks[1], (DEPTH, DIM, 3 * INNER)), 'q_scale': jnp.ones((DEPTH, DIM_HEAD), jnp.float32), 'k_scale': jnp.ones((DEPTH, DIM_HEAD), jnp.float32), 'Wo': init(ks[2], (DEPTH, INNER, DIM)), 'ln_g': jnp.ones((DEPTH, DIM), jnp.float32), 'ln_b': jnp.zeros((DEPTH, DIM), jnp.float32), 'W1': init(ks[3], (DEPTH, DIM, 2 * DIM_INNER)), 'b1': jnp.zeros((DEPTH, 2 * DIM_INNER), jnp.float32), 'W2': init(ks[4], (DEPTH, DIM_INNER, DIM)), 'b2': jnp.zeros((DEPTH, DIM), jnp.float32)}
    _L0_ffn_in = _L0_ffn_setup()
    _d = {'L0_attn_x': _L0_attn_in['x'], 'L0_attn_W_kv_down': _L0_attn_in['W_kv_down'], 'L0_attn_W_k_up': _L0_attn_in['W_k_up'], 'L0_attn_W_v_up': _L0_attn_in['W_v_up'], 'L0_attn_W_q': _L0_attn_in['W_q'], 'L0_attn_W_q_rope': _L0_attn_in['W_q_rope'], 'L0_attn_W_k_rope': _L0_attn_in['W_k_rope'], 'L0_attn_W_o': _L0_attn_in['W_o'], 'L0_ffn_Wqkv': _L0_ffn_in['Wqkv'], 'L0_ffn_q_scale': _L0_ffn_in['q_scale'], 'L0_ffn_k_scale': _L0_ffn_in['k_scale'], 'L0_ffn_Wo': _L0_ffn_in['Wo'], 'L0_ffn_ln_g': _L0_ffn_in['ln_g'], 'L0_ffn_ln_b': _L0_ffn_in['ln_b'], 'L0_ffn_W1': _L0_ffn_in['W1'], 'L0_ffn_b1': _L0_ffn_in['b1'], 'L0_ffn_W2': _L0_ffn_in['W2'], 'L0_ffn_b2': _L0_ffn_in['b2']}
    _x0 = _d['L0_attn_x']
    _d['L0_attn_x'] = jax.random.normal(jax.random.fold_in(jax.random.key(seed), 1), (2, 1024, 128), dtype=_x0.dtype)
    del _x0
    return _d

def reference(L0_attn_x, L0_attn_W_kv_down, L0_attn_W_k_up, L0_attn_W_v_up, L0_attn_W_q, L0_attn_W_q_rope, L0_attn_W_k_rope, L0_attn_W_o, L0_ffn_Wqkv, L0_ffn_q_scale, L0_ffn_k_scale, L0_ffn_Wo, L0_ffn_ln_g, L0_ffn_ln_b, L0_ffn_W1, L0_ffn_b1, L0_ffn_W2, L0_ffn_b2):

    def _L0_attn_ref(x, W_kv_down, W_k_up, W_v_up, W_q, W_q_rope, W_k_rope, W_o):
        import jax, jax.numpy as jnp
        import numpy as np
        import math
        D_MODEL, D_C, D_R, NH = (128, 128, 32, 16)
        HD = D_MODEL // NH
        B, T = (2, 256)

        def _rope_tables(T, d_R):
            inv_freq = 1.0 / 10000.0 ** (jnp.arange(0, d_R, 2, dtype=jnp.float32) / d_R)
            t = jnp.arange(T, dtype=jnp.float32)
            freqs = jnp.outer(t, inv_freq)
            return (jnp.cos(freqs), jnp.sin(freqs))

        def _rotary_apply(x, cos, sin):
            d = x.shape[-1]
            x1, x2 = (x[..., :d // 2], x[..., d // 2:])
            return jnp.concatenate([x1 * cos - x2 * sin, x2 * cos + x1 * sin], axis=-1)
        Bb, Tt, _ = x.shape
        cos, sin = _rope_tables(Tt, D_R)
        cos = cos[None]
        sin = sin[None]
        c_kv = x @ W_kv_down
        k_rope = _rotary_apply(c_kv @ W_k_rope, cos, sin)
        k = (c_kv @ W_k_up).reshape(Bb, Tt, NH, HD)
        v = (c_kv @ W_v_up).reshape(Bb, Tt, NH, HD)
        q = (x @ W_q).reshape(Bb, Tt, NH, HD)
        q_rope = _rotary_apply(x @ W_q_rope, cos, sin)
        scale = math.sqrt(HD + D_R)
        scores = jnp.einsum('bqhd,bkhd->bhqk', q, k)
        scores = scores + jnp.einsum('bqr,bkr->bqk', q_rope, k_rope)[:, None]
        scores = scores / scale
        causal = jnp.triu(jnp.ones((Tt, Tt), dtype=bool), k=1)
        scores = jnp.where(causal[None, None], -jnp.inf, scores)
        w = jax.nn.softmax(scores, axis=-1)
        attn = jnp.einsum('bhqk,bkhd->bqhd', w, v).reshape(Bb, Tt, D_MODEL)
        return attn @ W_o

    def _L0_ffn_ref(x, Wqkv, q_scale, k_scale, Wo, ln_g, ln_b, W1, b1, W2, b2):
        import jax, jax.numpy as jnp
        import numpy as np
        DIM = 128
        DEPTH = 6
        HEADS = 16
        DIM_HEAD = 64
        WINDOW = 32
        INNER = HEADS * DIM_HEAD
        DIM_INNER = int(DIM * 4 * 2 / 3)
        QK_SCALE = 8.0

        def shift_tokens(t):
            a, s = jnp.split(t, 2, -1)
            s = jnp.pad(s, ((0, 0), (1, 0), (0, 0)))[:, :-1]
            return jnp.concatenate([a, s], -1)

        def l2norm(t):
            return t / jnp.maximum(jnp.linalg.norm(t, axis=-1, keepdims=True), 1e-12)

        def rotate_half(x):
            x1, x2 = jnp.split(x, 2, -1)
            return jnp.concatenate([-x2, x1], -1)

        def rotary_tables(n):
            half = jnp.arange(0, DIM_HEAD, 2, dtype=jnp.float32)
            inv_freq = 1.0 / 10000.0 ** (half / DIM_HEAD)
            t = jnp.arange(n, dtype=jnp.float32)
            freqs = t[:, None] * inv_freq[None, :]
            freqs = jnp.concatenate([freqs, freqs], -1)
            base_scale = (half + 0.4 * DIM_HEAD) / (1.4 * DIM_HEAD)
            power = (t - n // 2) / (WINDOW // 2)
            scale = base_scale[None, :] ** power[:, None]
            scale = jnp.concatenate([scale, scale], -1)
            return (freqs, scale)

        def local_attention(q, k, v):
            b, h, n, d = q.shape
            w = WINDOW
            nw = n // w
            bq = q.reshape(b, h, nw, w, d)
            bk = k.reshape(b, h, nw, w, d)
            bv = v.reshape(b, h, nw, w, d)

            def look(t):
                p = jnp.pad(t, ((0, 0), (0, 0), (1, 0), (0, 0), (0, 0)))
                return jnp.concatenate([p[:, :, :nw], p[:, :, 1:]], axis=3)
            bk2, bv2 = (look(bk), look(bv))
            seq = jnp.arange(n).reshape(nw, w)
            seq_p = jnp.pad(seq, ((1, 0), (0, 0)), constant_values=-1)
            jt = jnp.concatenate([seq_p[:nw], seq_p[1:]], axis=1)
            it = seq[:, :, None]
            jb = jt[:, None, :]
            mask = (it < jb) | (it > jb + w) | (jb == -1)
            sim = jnp.einsum('bhwie,bhwje->bhwij', bq, bk2) * QK_SCALE
            sim = jnp.where(mask, -jnp.finfo(sim.dtype).max, sim)
            attn = jax.nn.softmax(sim, -1)
            out = jnp.einsum('bhwij,bhwje->bhwie', attn, bv2)
            return out.reshape(b, h, n, d)

        def attn_layer(x, Wqkv, qs, ksc, Wo):
            b, n, _ = x.shape
            qkv = x @ Wqkv
            q, k, v = jnp.split(qkv, 3, -1)
            sh = lambda t: t.reshape(b, n, HEADS, DIM_HEAD).transpose(0, 2, 1, 3)
            q, k, v = (sh(q), sh(k), sh(v))
            q = l2norm(q) * qs
            k = l2norm(k) * ksc
            freqs, scale = rotary_tables(n)
            cos, sin = (jnp.cos(freqs), jnp.sin(freqs))
            q = q * cos * scale + rotate_half(q) * sin * scale
            inv = 1.0 / scale
            k = k * cos * inv + rotate_half(k) * sin * inv
            out = local_attention(q, k, v)
            out = out.transpose(0, 2, 1, 3).reshape(b, n, INNER)
            return out @ Wo

        def ffn_layer(x, g, bln, W1, b1, W2, b2):
            mu = x.mean(-1, keepdims=True)
            var = ((x - mu) ** 2).mean(-1, keepdims=True)
            xn = (x - mu) / jnp.sqrt(var + 1e-05) * g + bln
            hg = xn @ W1 + b1
            a, gate = jnp.split(hg, 2, -1)
            return a * jax.nn.gelu(gate, approximate=False) @ W2 + b2
        for i in range(DEPTH):
            x = attn_layer(shift_tokens(x), Wqkv[i], q_scale[i], k_scale[i], Wo[i]) + x
            x = ffn_layer(shift_tokens(x), ln_g[i], ln_b[i], W1[i], b1[i], W2[i], b2[i]) + x
        return x
    x = L0_attn_x
    x = x + 0.5 * _L0_ffn_ref(_layernorm(x, axis=-1), L0_ffn_Wqkv, L0_ffn_q_scale, L0_ffn_k_scale, L0_ffn_Wo, L0_ffn_ln_g, L0_ffn_ln_b, L0_ffn_W1, L0_ffn_b1, L0_ffn_W2, L0_ffn_b2)
    x = x + _L0_attn_ref(_layernorm(x, axis=-1), L0_attn_W_kv_down, L0_attn_W_k_up, L0_attn_W_v_up, L0_attn_W_q, L0_attn_W_q_rope, L0_attn_W_k_rope, L0_attn_W_o)
    x = x + 0.5 * _L0_ffn_ref(_layernorm(x, axis=-1), L0_ffn_Wqkv, L0_ffn_q_scale, L0_ffn_k_scale, L0_ffn_Wo, L0_ffn_ln_g, L0_ffn_ln_b, L0_ffn_W1, L0_ffn_b1, L0_ffn_W2, L0_ffn_b2)
    return x

_drawn_inputs = setup_inputs


def setup_inputs(seed=0):
    import zlib

    import numpy as np

    out = dict(_drawn_inputs(seed))
    spreads = {'L0_ffn_q_scale': (1.0, 0.6),
     'L0_ffn_k_scale': (1.0, 0.6),
     'L0_ffn_ln_g': (1.0, 0.6),
     'L0_ffn_ln_b': (0.0, 0.8),
     'L0_ffn_b1': (0.0, 0.8),
     'L0_ffn_b2': (0.0, 0.1)}
    factors = {'L0_ffn_W1': 3.145, 'L0_ffn_W2': 3.087, 'L0_attn_W_k_up': 3.212, 'L0_attn_W_q': 3.325}
    for name, (base, spread) in spreads.items():
        noise = np.random.default_rng([zlib.crc32(name.encode()), seed]).standard_normal(out[name].shape)
        drawn = base * np.exp(spread * noise) if base else spread * noise
        out[name] = jnp.asarray(drawn.astype(out[name].dtype))
    for name, factor in factors.items():
        out[name] = (out[name] * factor).astype(out[name].dtype)
    return out
```

```python
import concourse.bass as bass
from concourse import mybir
from contextlib import ExitStack
import numpy as np

B, T, D = 2, 1024, 128
P = 128
NT = T // P
DEPTH, HEADS, DH, WIN = 6, 16, 64, 32
INNER = HEADS * DH
PAIRS = HEADS // 2
NW = P // WIN
F = int(D * 4 * 2 / 3)
FP = [min(P, F - P * j) for j in range(-(-F // P))]
NF = len(FP)
UNITS = B * NT
CHUNK = 512
CHUNKS = B * T // CHUNK
QK_SCALE = 8.0
MA_H, MA_D, MA_R = 16, 8, 32
MA_SCALE = float(MA_D + MA_R) ** -0.5
NEG = -3.0e38
CREDIT = 4


def macaron_program(nc, x_in, wqkv_in, wo_in, w1_in, w2_in, vec_in, scale_in, ma_down_in, ma_up_in,
                    ma_q_in, ma_o_in, rotary_in, mask_in, square_in, ma_rotary_in, out):
    fp32, bf16, i32 = mybir.dt.float32, mybir.dt.bfloat16, mybir.dt.int32
    ALU, ACT, AX = mybir.AluOpType, mybir.ActivationFunctionType, mybir.AxisListType
    ctx = ExitStack()
    with ctx:
        def sb(name, shape, dt=fp32):
            return ctx.enter_context(nc.sbuf_tensor(name, shape, dt))

        def sem(name):
            return ctx.enter_context(nc.semaphore(name))

        x_tok = sb("x_tok", [P, B * NT, D])
        X = sb("X", [P, B, T + 4])
        Y = sb("Y", [P, B, T + 4])
        squares = sb("squares", [P, 3, P])
        ident = squares[:, 0, :]
        ident_b = sb("ident_b", [P, P], bf16)
        causal_b = sb("causal_b", [P, 4 * P], bf16)
        band_b = sb("band_b", [P, NT, 2 * WIN], bf16)
        ones = sb("ones", [P, P])
        rotary = sb("rotary", [P, NT, 4, DH])
        mean_w = sb("mean_w", [P, P])
        ln_a = sb("ln_a", [P, B * NT])
        ln_s = [sb(f"ln_s{i}", [P, B * NT]) for i in range(4)]

        pool = sb("pool", [P, 40000])
        at = [0]

        def cut(*shape):
            n = int(np.prod(shape))
            v = pool[:, at[0]:at[0] + n]
            at[0] += n
            names = "abcd"[:len(shape)]
            if len(shape) > 1:
                v = v.rearrange(f"p ({' '.join(names)}) -> p {' '.join(names)}",
                                **dict(zip(names[1:], shape[1:])))
            return v

        wqkv = cut(3 * INNER)
        wo = cut(PAIRS, D)
        w1 = cut(2 * F)
        w2 = cut(NF, D)
        vec = cut(2 * NF + 3)
        scales = cut(4 * DH)
        turn = cut(NT, 4, DH)
        xs = cut(2, P)
        sq = cut(2 * INNER)
        qn = cut(2, HEADS, DH)
        by_cos = cut(2, HEADS, DH)
        rot = cut(2, HEADS, DH)
        ss = cut(2 * HEADS)
        nwt = [cut(2 * HEADS) for _ in range(4)]
        qT = cut(PAIRS, P)
        kT = [cut(PAIRS, 2, WIN + P) for _ in range(2)]
        V = [cut(INNER) for _ in range(4)]
        v_last = [cut(INNER) for _ in range(2)]
        S = cut(HEADS, 2 * WIN)
        top, total, over = cut(HEADS), cut(HEADS), cut(HEADS)
        pT = cut(HEADS, P)
        pT_last = cut(HEADS, WIN)
        oT = cut(PAIRS, P)
        kT_end = at[0]
        xc, fsq, xn = cut(CHUNK), cut(CHUNK), cut(CHUNK)
        diag = cut(CHUNK // P, P)
        gel = [cut(CHUNK) for _ in range(2)]
        hid = [cut(CHUNK) for _ in range(NF)]
        var = [cut(CHUNK // P) for _ in range(4)]
        layers_end = at[0]
        at[0] = 0
        ln_x = cut(B * NT, D)
        ln_q = cut(B * NT, D)

        at[0] = 0
        g_x, g_c = cut(T), cut(T)
        g_qT, g_kT = cut(MA_H // 2, T), cut(MA_H // 2, T)
        g_v = cut(NT, MA_H, WIN)
        g_q, g_k = [cut(MA_H, 64) for _ in range(2)], [cut(MA_H, 64) for _ in range(2)]
        g_rot = [cut(4, MA_R) for _ in range(2)]
        g_new = [cut(2, MA_R) for _ in range(2)]
        g_p, g_pT = [cut(T) for _ in range(2)], [cut(T) for _ in range(2)]
        g_top = [cut(1) for _ in range(2)]
        g_o, g_over, g_on = cut(4 * P), cut(4 * P), cut(4 * P)
        g_down, g_up, g_qw, g_wo = cut(D), cut(2 * D + MA_R), cut(D + MA_R), cut(4, D)
        g_tab = cut(NT, 2, MA_R // 2)

        psum = ctx.enter_context(nc.psum_tensor("psum", [P, 4096], fp32))

        def bank(b, n=1):
            return psum[:, 512 * b:512 * (b + n)]

        w_const, w_attn, w_ffn = sem("w_const"), sem("w_attn"), sem("w_ffn")
        kept = [sem("kept0"), sem("kept1")]
        xs_ready, qk_ready, v_ready = sem("xs_ready"), sem("qk_ready"), sem("v_ready")
        sq_ready, qn_ready, cos_ready = sem("sq_ready"), sem("qn_ready"), sem("cos_ready")
        sin_ready, rot_ready, turn_ready = sem("sin_ready"), sem("rot_ready"), sem("turn_ready")
        t_ready, t_out, v_out = sem("t_ready"), sem("t_out"), sem("v_out")
        k_kept, s_ready, s_taken, p_ready = sem("k_kept"), sem("s_ready"), sem("s_taken"), sem("p_ready")
        over_ready, pn_ready, pt_ready = sem("over_ready"), sem("pn_ready"), sem("pt_ready")
        o_ready, o_out, wo_ready, y_ready = sem("o_ready"), sem("o_out"), sem("wo_ready"), sem("y_ready")
        norm_step, soft_step = sem("norm_step"), sem("soft_step")
        mu_ready, xc_ready, fsq_ready, var_ready = sem("mu_ready"), sem("xc_ready"), sem("fsq_ready"), sem("var_ready")
        diag_ready, rb_ready, xn_ready = sem("diag_ready"), sem("rb_ready"), sem("xn_ready")
        w1_ready, gel_ready, hid_ready = sem("w1_ready"), sem("gel_ready"), sem("hid_ready")
        w2_ready, x_ready, var_step, aff_step = sem("w2_ready"), sem("x_ready"), sem("var_step"), sem("aff_step")
        set_up, ln_step, ln_ready, ln_T = sem("set_up"), sem("ln_step"), sem("ln_ready"), sem("ln_T")
        flat_ready, flat_T = sem("flat_ready"), sem("flat_T")
        stored = sem("stored")
        gx_ready, gc_ready, gc_out = sem("gx_ready"), sem("gc_ready"), sem("gc_out")
        proj_ready, rot_step, gq_ready = sem("proj_ready"), sem("rot_step"), sem("gq_ready")
        gk_ready, gT_ready, gT_a, gT_v = sem("gk_ready"), sem("gT_ready"), sem("gT_a"), sem("gT_v")
        gs_ready, gtop_ready, gp_ready = sem("gs_ready"), sem("gtop_ready"), sem("gp_ready")
        gt_ready, gt_a, gt_v, gpv_ready = sem("gt_ready"), sem("gt_a"), sem("gt_v"), sem("gpv_ready")
        go_out, gsum_ready, gon_step, gon_ready = sem("go_out"), sem("gsum_ready"), sem("gon_step"), sem("gon_ready")
        gwo_ready, gx_added, w_global, g_zero = sem("gwo_ready"), sem("gx_added"), sem("w_global"), sem("g_zero")
        passed_sp, passed_pool = sem("passed_sp"), sem("passed_pool")

        counted = {
            "tensor": [gc_ready, proj_ready, gT_ready, gs_ready, gt_ready, gpv_ready, gsum_ready, gwo_ready, qk_ready, v_ready, t_ready, s_ready, o_ready, wo_ready, mu_ready, var_ready,
                       rb_ready, w1_ready, w2_ready],
            "scalar": [gx_ready, gc_out, gk_ready, gT_a, gp_ready, gt_a, go_out, xs_ready, sq_ready, v_out, t_out, p_ready, o_out, fsq_ready, gel_ready],
            "vector": [rot_step, gq_ready, gT_v, gtop_ready, gt_v, gon_step, gon_ready, gx_added, qn_ready, cos_ready, s_taken, over_ready, pt_ready, y_ready, norm_step, soft_step,
                       xc_ready, diag_ready, xn_ready, hid_ready, x_ready, var_step, aff_step],
            "gpsimd": [sin_ready, rot_ready, turn_ready, k_kept, pn_ready],
        }

        def done(unit, per=1, part=0):
            return unit * per + part + 1 + CREDIT

        def kept_by(layer, i, n):
            return (layer * NT + 2 * i + n // 2 + 1) * 16

        def plain(eng):
            eng.sem_inc(passed_sp if eng is nc.sync else passed_pool, 1)

        def rsqrt(v, x, tmp, step, first, op0, c0, op1, c1):
            u, h, a, y = tmp
            n = [0]

            def link(ins):
                ins.then_inc(step, 1)
                n[0] += 1
                v.wait_ge(step, first + n[0])

            link(v.tensor_scalar(u, x, c0, c1, op0, op1))
            link(v.tensor_scalar(h, u, -0.5, None, ALU.mult))
            link(v.tensor_scalar(y.bitcast(i32), u.bitcast(i32), -0.5, 1597463007.0, ALU.mult, ALU.add))
            for _ in range(3):
                link(v.tensor_tensor(a, y, h, ALU.mult))
                link(v.tensor_tensor(a, a, y, ALU.mult))
                link(v.scalar_tensor_tensor(y, a, 1.5, y, ALU.add, ALU.mult))
        RSQRT = 12

        with nc.Block() as block:
            @block.sync
            def _(sp):
                sp.dma_start(x_tok[:], x_in.rearrange("b (t p) d -> p (b t) d", p=P)).then_inc(w_const, 16)
                sp.dma_start(squares[:], square_in).then_inc(w_const, 16)
                sp.dma_start(rotary[:], rotary_in).then_inc(w_const, 16)
                sp.dma_start(pool[:, layers_end:layers_end + NT * 2 * WIN], mask_in).then_inc(w_const, 16)
                sp.wait_ge(w_const, 64)

            @block.vector
            def _(v):
                for s in counted["vector"]:
                    v.sem_inc(s, CREDIT)
                v.wait_ge(w_const, 64)
                v.tensor_copy(ident_b[:], ident)
                v.memset(causal_b[:, 0:3 * P], 0.0)
                v.tensor_copy(causal_b[:, 3 * P:4 * P], squares[:, 2, :])
                v.tensor_copy(band_b[:].rearrange("p t k -> p (t k)"),
                              pool[:, layers_end:layers_end + NT * 2 * WIN]).then_inc(set_up, 1)
                v.memset(ones[:], 1.0)
                v.memset(mean_w[:], 1.0 / D).then_inc(set_up, 1)

            @block.scalar
            def _(a):
                for s in counted["scalar"]:
                    a.sem_inc(s, CREDIT)

            @block.tensor
            def _(pe):
                for s in counted["tensor"]:
                    pe.sem_inc(s, CREDIT)

            @block.gpsimd
            def _(g):
                for s in counted["gpsimd"]:
                    g.sem_inc(s, CREDIT)
                g.memset(X[:], 0.0)
                g.memset(Y[:], 0.0).then_inc(set_up, 1)

        def zero_blocks():
            with nc.Block() as block:
                @block.gpsimd
                def _(g):
                    g.memset(kT[0], 0.0)
                    g.memset(kT[1], 0.0)
                    g.memset(v_last[0], 0.0)
                    g.memset(v_last[1], 0.0).then_inc(set_up, 1)

                @block.vector
                def _(v):
                    v.memset(Y[64:128, :, 0:1], 0.0)
                    v.memset(pT, 0.0)
                    v.memset(pT_last, 0.0)
                    for i in range(4):
                        last = v.memset(V[i], 0.0)
                    last.then_inc(set_up, 1)

        ln_count = [0]

        def layer_norm_tokens(to_skewed):
            r = ln_count[0]
            ln_count[0] += 1
            base = r * (RSQRT + 5)
            with nc.Block() as block:
                @block.vector
                def _(v):
                    n = [base]

                    def link(ins):
                        ins.then_inc(ln_step, 1)
                        n[0] += 1
                        v.wait_ge(ln_step, n[0])

                    wide = [P, B * NT, D]
                    link(v.tensor_reduce(ln_a[:], x_tok[:], AX.X, ALU.add))
                    link(v.tensor_scalar(ln_a[:], ln_a[:], -1.0 / D, None, ALU.mult))
                    link(v.tensor_tensor(ln_x, x_tok[:], ln_a[:].unsqueeze(2).broadcast_to(wide), ALU.add))
                    link(v.tensor_tensor(ln_q, ln_x, ln_x, ALU.mult))
                    link(v.tensor_reduce(ln_a[:], ln_q, AX.X, ALU.add))
                    rsqrt(v, ln_a[:], [t[:] for t in ln_s], ln_step, n[0], ALU.mult, 1.0 / D, ALU.add, 1e-5)
                    v.tensor_tensor(ln_x, ln_x, ln_s[3][:].unsqueeze(2).broadcast_to(wide),
                                    ALU.mult).then_inc(ln_ready, 1)

                @block.tensor
                def _(pe):
                    pe.wait_ge(ln_ready, r + 1)
                    for j in range(B * NT):
                        t = pe.transpose(psum[:, P * j:P * j + P], ln_x[:, j, :], ident)
                        if j % 4 == 3:
                            t.then_inc(ln_T, 1)

                @block.scalar
                def _(a):
                    for j in range(4):
                        a.wait_ge(ln_T, 4 * r + j + 1)
                        b, c = j // 2, CHUNK * (j % 2)
                        if to_skewed:
                            a.copy(X[0:64, b, c:c + CHUNK], bank(j)[0:64, :])
                            a.copy(X[64:128, b, c + 1:c + 1 + CHUNK], bank(j)[64:128, :])
                        else:
                            a.copy(Y[:, b, c:c + CHUNK], bank(j))

        def attention(eng_name, eng, layer, U0, step, half):
            for k in range(3):
                step(0, k, lambda d, k=k: k - d >= 0)
            with eng.Fori(0, 3) as i:
                for k in range(3, 7):
                    step(i, k, lambda d: True)
            for k in range(3, 7):
                step(3, k, lambda d, k=k: 12 + k - d < UNITS)

        def layers(half):
            with nc.Block() as block:
                L0 = DEPTH * half

                @block.sync
                def _(sp):
                    with sp.Fori(0, DEPTH) as l:
                        U0, C0 = (l + L0) * UNITS, (l + L0) * CHUNKS
                        sp.wait_ge(wo_ready, done(U0 - 1))
                        plain(sp)
                        sp.wait_ge(turn_ready, done(l + L0 - 1))
                        plain(sp)
                        sp.dma_start(wqkv, wqkv_in[bass.ds(l, 1)].rearrange("a p n -> p (a n)")).then_inc(w_attn, 16)
                        sp.dma_start(wo, wo_in[bass.ds(l, 1)].rearrange("a p c n -> p (a c) n")).then_inc(w_attn, 16)
                        sp.dma_start(scales, scale_in[bass.ds(l, 1)].rearrange("a p n -> p (a n)")).then_inc(w_attn, 16)
                        sp.wait_ge(x_ready, done(C0 - 1))
                        plain(sp)
                        sp.dma_start(w1, w1_in[bass.ds(l, 1)].rearrange("a p n -> p (a n)")).then_inc(w_ffn, 16)
                        sp.dma_start(w2, w2_in[bass.ds(l, 1)].rearrange("a p c n -> p (a c) n")).then_inc(w_ffn, 16)
                        sp.dma_start(vec, vec_in[bass.ds(l, 1)].rearrange("a p n -> p (a n)")).then_inc(w_ffn, 16)

                        def step(i, k, has):
                            U = U0 + 4 * i + k
                            if has(0):
                                sp.wait_ge(o_ready, done(U - 2))
                                sp.wait_ge(v_out, done(U - 2))
                                plain(sp)
                                sp.dma_start(v_last[k % 2][96:128, :],
                                             V[(k - 2) % 4][96:128, :]).then_inc(kept[k % 2], 16)

                        attention("sync", sp, l, U0, step, half)

                @block.tensor
                def _(pe):
                    with pe.Fori(0, DEPTH) as l:
                        U0, C0 = (l + L0) * UNITS, (l + L0) * CHUNKS

                        def step(i, k, has):
                            U = U0 + 4 * i + k
                            if has(0):
                                if k == 0:
                                    pe.wait_ge(w_attn, (l + L0 + 1) * 48)
                                pe.wait_ge(xs_ready, done(U))
                                pe.wait_ge(qn_ready, done(U - 1))
                                for j in range(4):
                                    last = pe.matmul(bank(j), xs[:, k % 2, :], wqkv[:, 512 * j:512 * j + 512],
                                                     start=True, stop=True)
                                last.then_inc(qk_ready, 1)
                            if has(3):
                                pe.wait_ge(o_out, done(U - 3))
                                for c in range(PAIRS):
                                    last = pe.matmul(bank(6)[:, 0:P], wo[:, c, :], oT[:, c, :],
                                                     start=(c == 0), stop=(c == PAIRS - 1))
                                last.then_inc(wo_ready, 1)
                            if has(0):
                                pe.wait_ge(s_taken, done(U - 2))
                                if not has(2):
                                    pe.wait_ge(v_out, done(U - 1))
                                for j in range(2):
                                    last = pe.matmul(bank(4 + j), xs[:, k % 2, :],
                                                     wqkv[:, 2 * INNER + 512 * j:2 * INNER + 512 * j + 512],
                                                     start=True, stop=True)
                                last.then_inc(v_ready, 1)
                            if has(3):
                                pe.wait_ge(y_ready, done(U - 3))
                            if has(1):
                                pe.wait_ge(rot_ready, done(U - 1))
                                for p in range(4):
                                    if p >= 2:
                                        pe.wait_ge(t_out, done(U - 1, 4, p - 2))
                                    for j in range(4):
                                        c = 4 * (p % 2) + j
                                        last = pe.transpose(bank(7 - p % 2)[:, P * j:P * j + P],
                                                            rot[:, p // 2, 2 * c:2 * c + 2, :], ident)
                                    last.then_inc(t_ready, 1)
                                pe.wait_ge(k_kept, done(U - 1))
                                pe.wait_ge(t_out, done(U - 1, 4, 3))
                                pe.wait_ge(v_out, done(U if has(0) else U - 1))
                                if not has(0):
                                    pe.wait_ge(s_taken, done(U - 2))
                                t = 2 * i + (k - 1) // 2
                                band = band_b[:, bass.ds(t, 1), :].broadcast_to([P, HEADS // 2, 2 * WIN])
                                for j in range(2):
                                    pe.matmul(bank(4 + j), ident_b[:], band, start=True, stop=False)
                                for c in range(PAIRS):
                                    for w in range(NW):
                                        o = bank(4 + c // 4)[WIN * w:WIN * w + WIN, P * (c % 4):P * (c % 4) + P]
                                        last = pe.matmul(o, qT[:, c, WIN * w:WIN * w + WIN],
                                                         kT[(k - 1) % 2][:, c, :, WIN * w:WIN * w + 2 * WIN],
                                                         start=False, stop=(c % 4 == 3))
                                last.then_inc(s_ready, 1)
                            if has(2):
                                pe.wait_ge(pt_ready, done(U - 2))
                                pe.wait_ge(kept[k % 2], kept_by(l + L0, i, k - 2))
                                for h in range(HEADS):
                                    r = 64 * (h % 2)
                                    o = bank(6 + h // 8)[r:r + 64, P * (h // 2 % 4):P * (h // 2 % 4) + P]
                                    pe.matmul(o, V[(k - 2) % 4][:, DH * h:DH * h + DH], pT[:, h, :],
                                              start=True, stop=False)
                                    last = pe.matmul(o[:, 0:WIN], v_last[k % 2][:, DH * h:DH * h + DH],
                                                     pT_last[:, h, :], start=False, stop=True)
                                last.then_inc(o_ready, 1)

                        attention("tensor", pe, l, U0, step, half)

                        def mean(c):
                            C = C0 + c
                            pe.wait_ge(y_ready, done(U0 + 2 * (4 * (c // 2) + 3) + c % 2))
                            pe.matmul(bank(4), mean_w[:], Y[:, c % 2, CHUNK * (c // 2):CHUNK * (c // 2) + CHUNK],
                                      start=True, stop=True).then_inc(mu_ready, 1)

                        def variance(c):
                            pe.wait_ge(fsq_ready, done(C0 + c))
                            for j in range(CHUNK // P):
                                last = pe.matmul(bank(5)[:, j:j + 1], fsq[:, P * j:P * j + P], mean_w[:, 0:1],
                                                 start=True, stop=True)
                            last.then_inc(var_ready, 1)

                        def spread(c):
                            pe.wait_ge(diag_ready, done(C0 + c))
                            if c == 0:
                                pe.wait_ge(y_ready, done(U0 + UNITS - 1))
                            pe.matmul(bank(6), ones[:], diag.rearrange("p a b -> p (a b)"),
                                      start=True, stop=True).then_inc(rb_ready, 1)

                        def up(c, j):
                            C = C0 + c
                            if j == 0:
                                pe.wait_ge(xn_ready, done(C))
                            pe.wait_ge(hid_ready, done(C, NF, j - 2))
                            m = FP[j]
                            pe.matmul(bank(2 * (j % 2))[0:m, :], w1[:, P * j:P * j + m], xn, start=True, stop=True)
                            pe.matmul(bank(2 * (j % 2) + 1)[0:m, :], w1[:, F + P * j:F + P * j + m], xn,
                                      start=True, stop=True).then_inc(w1_ready, 1)

                        def down(c):
                            C = C0 + c
                            pe.wait_ge(x_ready, done(C - 1))
                            for j in range(NF):
                                pe.wait_ge(hid_ready, done(C, NF, j))
                                last = pe.matmul(bank(7), w2[0:FP[j], j, :], hid[j][0:FP[j], :],
                                                 start=(j == 0), stop=(j == NF - 1))
                            last.then_inc(w2_ready, 1)

                        pe.wait_ge(w_ffn, (l + L0 + 1) * 48)
                        mean(0)
                        variance(0)
                        spread(0)
                        for c in range(CHUNKS):
                            more = c + 1 < CHUNKS
                            if more:
                                mean(c + 1)
                            up(c, 0)
                            up(c, 1)
                            if more:
                                variance(c + 1)
                            up(c, 2)
                            if more:
                                spread(c + 1)
                            down(c)

                @block.scalar
                def _(a):
                    with a.Fori(0, DEPTH) as l:
                        U0, C0 = (l + L0) * UNITS, (l + L0) * CHUNKS

                        def take(i, n):
                            U = U0 + 4 * i + n
                            a.wait_ge(v_ready, done(U - 2))
                            c = n if isinstance(i, int) and 4 * i + n < 2 else CHUNKS - 1
                            a.wait_ge(x_ready, done(C0 - CHUNKS + c))
                            t = 2 * i + n // 2
                            a.copy(xs[:, n % 2, :], X[:, n % 2, bass.ds(t * P, P)]).then_inc(xs_ready, 1)

                        take(0, 0)

                        def step(i, k, has):
                            U = U0 + 4 * i + k
                            if has(0):
                                a.wait_ge(qk_ready, done(U))
                                a.wait_ge(qn_ready, done(U - 1))
                                a.activation(sq, bank(0, 4), ACT.Square).then_inc(sq_ready, 1)
                            if has(-1):
                                take(i, k + 1)
                            if has(0):
                                a.wait_ge(v_ready, done(U))
                                a.wait_ge(o_ready, done(U - 4))
                                if k >= 2:
                                    a.wait_ge(kept[k % 2], kept_by(l + L0, i, k - 2))
                                a.copy(V[k % 4], bank(4, 2)).then_inc(v_out, 1)
                            if has(1):
                                s = (k - 1) % 2
                                a.wait_ge(s_ready, done(U - 2))
                                for p in range(4):
                                    a.wait_ge(t_ready, done(U - 1, 4, p))
                                    if p < 2:
                                        a.copy(qT[:, 4 * p:4 * p + 4, :].rearrange("p c t -> p (c t)"),
                                               bank(7 - p)).then_inc(t_out, 1)
                                        continue
                                    if p == 2:
                                        a.wait_ge(k_kept, done(U - 1))
                                    c = 4 * (p - 2)
                                    for r in range(2):
                                        last = a.copy(kT[s][64 * r:64 * r + 64, c:c + 4, r, WIN:WIN + P],
                                                      bank(7 - p % 2)[64 * r:64 * r + 64, :]
                                                      .rearrange("p (c t) -> p c t", c=4))
                                    last.then_inc(t_out, 1)
                                a.wait_ge(s_taken, done(U - 1))
                                a.activation(S, S, ACT.Exp).then_inc(p_ready, 1)
                            if has(2):
                                a.wait_ge(o_ready, done(U - 2))
                                a.wait_ge(wo_ready, done(U - 3))
                                a.copy(oT.rearrange("p c t -> p (c t)"), bank(6, 2)).then_inc(o_out, 1)

                        attention("scalar", a, l, U0, step, half)

                        def squares_of(c):
                            a.wait_ge(xc_ready, done(C0 + c))
                            a.activation(fsq, xc, ACT.Square).then_inc(fsq_ready, 1)

                        a.wait_ge(w_ffn, (l + L0 + 1) * 48)
                        squares_of(0)
                        for c in range(CHUNKS):
                            if c + 1 < CHUNKS:
                                squares_of(c + 1)
                            for j in range(NF):
                                C = C0 + c
                                a.wait_ge(w1_ready, done(C, NF, j))
                                a.wait_ge(hid_ready, done(C, NF, j - 2))
                                m = FP[j]
                                a.activation(gel[j % 2][0:m, :], bank(2 * (j % 2) + 1)[0:m, :], ACT.Gelu,
                                             bias=vec[0:m, NF + j:NF + j + 1]).then_inc(gel_ready, 1)

                @block.gpsimd
                def _(g):
                    with g.Fori(0, DEPTH) as l:
                        U0, C0 = (l + L0) * UNITS, (l + L0) * CHUNKS
                        g.wait_ge(w_attn, (l + L0 + 1) * 48)
                        g.wait_ge(cos_ready, done(U0 - 1))
                        g.wait_ge(sin_ready, done(U0 - 1))
                        g.tensor_tensor(turn.rearrange("p t a e -> p t (a e)"),
                                        rotary[:].rearrange("p t a e -> p t (a e)"),
                                        scales.unsqueeze(1).broadcast_to([P, NT, 4 * DH]),
                                        ALU.mult).then_inc(turn_ready, 1)
                        g.wait_ge(turn_ready, done(l + L0))

                        def step(i, k, has):
                            U = U0 + 4 * i + k
                            if has(1):
                                g.wait_ge(s_ready, done(U - 3))
                                b = kT[(k - 1) % 2]
                                plain(g)
                                g.tensor_copy(b[:, :, :, 0:WIN], b[:, :, :, P:P + WIN]).then_inc(k_kept, 1)
                            if has(0):
                                t = 2 * i + k // 2
                                g.wait_ge(qn_ready, done(U))
                                g.wait_ge(t_ready, done(U - 1, 4, 3))
                                plain(g)
                                hd = DH // 2
                                for r in range(2):
                                    tab = turn[:, bass.ds(t, 1), 2:4, hd * r:hd * r + hd].rearrange(
                                        "p a q e -> p (a q) e").unsqueeze(2).broadcast_to([P, 2, HEADS, hd])
                                    last = g.tensor_tensor(rot[:, :, :, hd * r:hd * r + hd],
                                                           qn[:, :, :, hd * (1 - r):hd * (2 - r)], tab, ALU.mult)
                                last.then_inc(sin_ready, 1)
                                g.wait_ge(sin_ready, done(U))
                                g.wait_ge(cos_ready, done(U))
                                g.tensor_tensor(rot, rot, by_cos, ALU.add).then_inc(rot_ready, 1)
                            if has(1):
                                g.wait_ge(over_ready, done(U - 1))
                                g.tensor_tensor(S, S, over.unsqueeze(2).broadcast_to([P, HEADS, 2 * WIN]),
                                                ALU.mult).then_inc(pn_ready, 1)

                        attention("gpsimd", g, l, U0, step, half)

                @block.vector
                def _(v):
                    with v.Fori(0, DEPTH) as l:
                        U0, C0 = (l + L0) * UNITS, (l + L0) * CHUNKS

                        def step(i, k, has):
                            U = U0 + 4 * i + k
                            if has(2):
                                v.wait_ge(pn_ready, done(U - 2))
                                v.wait_ge(o_ready, done(U - 3))
                                for w in range(NW):
                                    rows = slice(WIN * w, WIN * w + WIN)
                                    v.transpose(pT[rows, :, rows], S[rows, :, WIN:2 * WIN])
                                    if w:
                                        v.transpose(pT[WIN * (w - 1):WIN * w, :, rows], S[rows, :, 0:WIN])
                                v.transpose(pT_last[96:128, :, :], S[0:WIN, :, 0:WIN]).then_inc(pt_ready, 1)
                            if has(3):
                                t = 2 * i + (k - 3) // 2
                                s = (k - 3) % 2
                                v.wait_ge(wo_ready, done(U - 3))
                                v.tensor_tensor(Y[0:64, s, bass.ds(t * P, P)], bank(6)[0:64, 0:P],
                                                X[0:64, s, bass.ds(t * P, P)], ALU.add)
                                v.tensor_tensor(Y[64:128, s, bass.ds(t * P + 1, P)], bank(6)[64:128, 0:P],
                                                X[64:128, s, bass.ds(t * P + 1, P)], ALU.add).then_inc(y_ready, 1)
                            if has(0):
                                t = 2 * i + k // 2
                                v.wait_ge(sq_ready, done(U))
                                v.tensor_reduce(ss, sq.rearrange("p (h e) -> p h e", e=DH), AX.X,
                                                ALU.add).then_inc(norm_step, 1)
                                v.wait_ge(norm_step, done(U, RSQRT + 1, 0))
                                rsqrt(v, ss, nwt, norm_step, done(U, RSQRT + 1, 0), ALU.max, 1e-24, ALU.mult, 1.0)
                                v.wait_ge(sin_ready, done(U - 1))
                                v.wait_ge(cos_ready, done(U - 1))
                                v.tensor_tensor(qn.rearrange("p q h e -> p (q h) e"),
                                                bank(0, 4).rearrange("p (h e) -> p h e", e=DH),
                                                nwt[3].unsqueeze(2).broadcast_to([P, 2 * HEADS, DH]),
                                                ALU.mult).then_inc(qn_ready, 1)
                            if has(1):
                                sc = bank(4, 2).rearrange("p (h e) -> p h e", e=2 * WIN)
                                v.wait_ge(s_ready, done(U - 1))
                                v.tensor_reduce(top, sc, AX.X, ALU.max).then_inc(soft_step, 1)
                                v.wait_ge(soft_step, done(U - 1, 2, 0))
                                if has(2):
                                    v.wait_ge(pt_ready, done(U - 2))
                                v.tensor_tensor(S, sc, top.unsqueeze(2).broadcast_to([P, HEADS, 2 * WIN]),
                                                ALU.subtract).then_inc(s_taken, 1)
                            if has(0):
                                if k == 0:
                                    v.wait_ge(turn_ready, done(l + L0))
                                v.wait_ge(qn_ready, done(U))
                                v.wait_ge(rot_ready, done(U - 1))
                                tab = turn[:, bass.ds(t, 1), 0:2, :].rearrange(
                                    "p a q e -> p (a q) e").unsqueeze(2).broadcast_to([P, 2, HEADS, DH])
                                v.tensor_tensor(by_cos, qn, tab, ALU.mult).then_inc(cos_ready, 1)
                            if has(1):
                                v.wait_ge(p_ready, done(U - 1))
                                v.tensor_reduce(total, S, AX.X, ALU.add).then_inc(soft_step, 1)
                                v.wait_ge(soft_step, done(U - 1, 2, 1))
                                v.reciprocal(over, total).then_inc(over_ready, 1)

                        attention("vector", v, l, U0, step, half)

                        def centre(c):
                            v.wait_ge(mu_ready, done(C0 + c))
                            v.tensor_tensor(xc, Y[:, c % 2, CHUNK * (c // 2):CHUNK * (c // 2) + CHUNK], bank(4),
                                            ALU.subtract).then_inc(xc_ready, 1)

                        def deviation(c):
                            v.wait_ge(var_ready, done(C0 + c))
                            rsqrt(v, bank(5)[:, 0:CHUNK // P], var, var_step, done(C0 + c, RSQRT, -1),
                                  ALU.mult, 1.0, ALU.add, 1e-5)
                            for j in range(CHUNK // P):
                                last = v.tensor_scalar(diag[:, j, :], ident, var[3][:, j:j + 1], None, ALU.mult)
                            last.then_inc(diag_ready, 1)

                        def normal(c):
                            v.wait_ge(rb_ready, done(C0 + c))
                            v.tensor_tensor(xn, xc, bank(6), ALU.mult).then_inc(aff_step, 1)
                            v.wait_ge(aff_step, done(C0 + c))
                            v.tensor_scalar(xn, xn, vec[:, 2 * NF:2 * NF + 1], vec[:, 2 * NF + 1:2 * NF + 2],
                                            ALU.mult, ALU.add).then_inc(xn_ready, 1)

                        def hidden(c, j):
                            m = FP[j]
                            v.wait_ge(gel_ready, done(C0 + c, NF, j))
                            v.wait_ge(w2_ready, done(C0 + c - 1))
                            v.scalar_tensor_tensor(hid[j][0:m, :], bank(2 * (j % 2))[0:m, :], vec[0:m, j:j + 1],
                                                   gel[j % 2][0:m, :], ALU.add, ALU.mult).then_inc(hid_ready, 1)

                        def result(c):
                            b, at0 = c % 2, CHUNK * (c // 2)
                            v.wait_ge(w2_ready, done(C0 + c))
                            for r in range(2):
                                rows = slice(64 * r, 64 * r + 64)
                                last = v.scalar_tensor_tensor(
                                    X[rows, b, at0 + r:at0 + r + CHUNK], bank(7)[rows, :],
                                    vec[rows, 2 * NF + 2:2 * NF + 3], Y[rows, b, at0 + r:at0 + r + CHUNK],
                                    ALU.add, ALU.add)
                            last.then_inc(x_ready, 1)

                        v.wait_ge(w_ffn, (l + L0 + 1) * 48)
                        centre(0)
                        deviation(0)
                        normal(0)
                        for c in range(CHUNKS):
                            more = c + 1 < CHUNKS
                            if more:
                                centre(c + 1)
                            hidden(c, 0)
                            if more:
                                deviation(c + 1)
                            hidden(c, 1)
                            hidden(c, 2)
                            if more:
                                normal(c + 1)
                            result(c)

        def add_half(half):
            with nc.Block() as block:
                @block.scalar
                def _(a):
                    for b in range(B):
                        a.copy(Y[0:64, b, 0:T], X[0:64, b, 0:T])
                        a.copy(Y[64:128, b, 0:T], X[64:128, b, 1:T + 1]).then_inc(flat_ready, 1)

                @block.tensor
                def _(pe):
                    for j in range(B * NT):
                        if j % NT == 0:
                            pe.wait_ge(flat_ready, B * half + j // NT + 1)
                        t = pe.transpose(psum[:, P * j:P * j + P], Y[:, j // NT, P * (j % NT):P * (j % NT) + P], ident)
                        if j % 4 == 3:
                            t.then_inc(flat_T, 1)

                @block.vector
                def _(v):
                    for j in range(4):
                        v.wait_ge(flat_T, 4 * half + j + 1)
                        x = x_tok[:, 4 * j:4 * j + 4, :].rearrange("p a d -> p (a d)")
                        v.scalar_tensor_tensor(x, bank(j), 0.5, x, ALU.mult, ALU.add)

        def global_attention():
            HS = NT * MA_H
            pieces = [(g, p) for g in range(HS) for p in range(g // MA_H // 4 + 1)]
            number = {gp: n for n, gp in enumerate(pieces)}
            by_a = [n % 2 == 0 for n in range(len(pieces))]

            def moved(b, n):
                own = [m for m in range(len(pieces)) if by_a[m] == by_a[n]]
                return (gt_a if by_a[n] else gt_v), done(b, len(own), own.index(n))

            def piece_out(eng, copy, b, g, p, n):
                t, h = divmod(g, MA_H)
                eng.wait_ge(gt_ready, done(b, len(pieces), n))
                if g >= 2:
                    eng.wait_ge(gpv_ready, done(b, HS, g - 2))
                m = P * min(4, t + 1 - 4 * p)
                return copy(g_pT[h % 2][:, 512 * p:512 * p + m], bank(4 + p)[:, 0:m])

            with nc.Block() as block:
                @block.sync
                def _(sp):
                    for a, b in ((g_down, ma_down_in), (g_up, ma_up_in), (g_qw, ma_q_in), (g_wo, ma_o_in),
                                 (g_tab, ma_rotary_in)):
                        sp.dma_start(a, b).then_inc(w_global, 16)

                @block.gpsimd
                def _(g):
                    for i in range(2):
                        g.memset(g_q[i], 0.0)
                        g.memset(g_k[i], 0.0)
                    g.memset(g_v, 0.0).then_inc(g_zero, 1)
                    g.wait_ge(g_zero, 1)
                    g.memset(g_v[:, :, :, MA_D:MA_D + 1], 1.0).then_inc(g_zero, 1)

                @block.tensor
                def _(pe):
                    pe.wait_ge(w_global, 80)
                    with pe.Fori(0, B) as b:
                        pe.wait_ge(gx_ready, done(b))
                        for j in range(2):
                            last = pe.matmul(bank(j), g_down, g_x[:, 512 * j:512 * j + 512], start=True, stop=True)
                        last.then_inc(gc_ready, 1)
                        pe.wait_ge(gc_out, done(b))

                        def project(t):
                            o, o2 = bank(2 * (t % 2)), bank(2 * (t % 2) + 1)
                            if t >= 2:
                                pe.wait_ge(gq_ready, done(b, NT, t - 2))
                                pe.wait_ge(gk_ready, done(b, NT, t - 2))
                            c = slice(P * t, P * t + P)
                            pe.matmul(o[:, 0:2 * D], g_c[:, c], g_up[:, 0:2 * D], start=True, stop=True)
                            pe.matmul(o2[:, 0:MA_R], g_c[:, c], g_up[:, 2 * D:2 * D + MA_R], start=True, stop=True)
                            pe.matmul(o2[:, MA_R:D + 2 * MA_R], g_x[:, c], g_qw,
                                      start=True, stop=True).then_inc(proj_ready, 1)

                        def turn_over(t):
                            pe.wait_ge(gq_ready, done(b, NT, t))
                            pe.wait_ge(gk_ready, done(b, NT, t))
                            for p in range(4):
                                if t:
                                    pe.wait_ge((gT_a, gT_v)[p % 2], done(b, 2 * NT, 2 * (t - 1) + p // 2))
                                for j in range(4):
                                    c = 4 * (p % 2) + j
                                    last = pe.transpose(bank(4 + p)[:, P * j:P * j + P],
                                                        (g_q, g_k)[p // 2][t % 2][:, 2 * c:2 * c + 2, :], ident)
                                last.then_inc(gT_ready, 1)

                        project(0)
                        for t in range(NT):
                            if t + 1 < NT:
                                project(t + 1)
                            turn_over(t)
                        pe.wait_ge(gT_a, done(b, 2 * NT, 2 * NT - 1))
                        pe.wait_ge(gT_v, done(b, 2 * NT, 2 * NT - 1))

                        def scores(g):
                            t, h = divmod(g, MA_H)
                            if g >= 2:
                                pe.wait_ge(gp_ready, done(b, HS, g - 2))
                            r, c = 64 * (h % 2), h // 2
                            q = g_qT[r:r + 64, c, P * t:P * t + P]
                            for j in range(t // 4 + 1):
                                n = min(P * (t + 1) - 512 * j, 512)
                                o = bank(2 * (h % 2) + j)
                                diagonal = 512 * j <= P * t < 512 * j + n
                                if diagonal:
                                    pe.matmul(o[:, 0:n], ident_b[:], causal_b[:, 512 - n:512],
                                              start=True, stop=False)
                                last = pe.matmul(o[:, 0:n], q, g_kT[r:r + 64, c, 512 * j:512 * j + n],
                                                 start=not diagonal, stop=True)
                            last.then_inc(gs_ready, 1)

                        def probabilities(g):
                            t, h = divmod(g, MA_H)
                            pe.wait_ge(gp_ready, done(b, HS, g))
                            for p in range(t // 4 + 1):
                                if (g - 1, p) in number:
                                    pe.wait_ge(*moved(b, number[g - 1, p]))
                                for j in range(min(4, t + 1 - 4 * p)):
                                    k = 4 * p + j
                                    last = pe.transpose(bank(4 + p)[:, P * j:P * j + P],
                                                        g_p[h % 2][:, P * k:P * k + P], ident)
                                last.then_inc(gt_ready, 1)

                        def values(g):
                            t, h = divmod(g, MA_H)
                            for p in range(t // 4 + 1):
                                pe.wait_ge(*moved(b, number[g, p]))
                            if h == 0 and t:
                                pe.wait_ge(go_out, done(b, NT, t - 1))
                            for k in range(t + 1):
                                last = pe.matmul(bank(6)[WIN * (h % 4):WIN * (h % 4) + WIN, P * (h // 4):P * (h // 4) + P],
                                                 g_v[:, k, h, :], g_pT[h % 2][:, P * k:P * k + P],
                                                 start=(k == 0), stop=(k == t))
                            last.then_inc(gpv_ready, 1)

                        def sums(t):
                            pe.wait_ge(go_out, done(b, NT, t))
                            if t:
                                pe.wait_ge(gx_added, done(b, NT, t - 1))
                            pe.matmul(bank(7), squares[:, 1, :], g_o, start=True, stop=True).then_inc(gsum_ready, 1)

                        def project_out(t):
                            pe.wait_ge(gon_ready, done(b, NT, t))
                            for j in range(4):
                                last = pe.matmul(bank(7)[:, 0:P], g_on[:, P * j:P * j + P], g_wo[:, j, :],
                                                 start=(j == 0), stop=(j == 3))
                            last.then_inc(gwo_ready, 1)

                        scores(0)
                        for g in range(HS + 1):
                            t, h = divmod(g, MA_H)
                            if g + 1 < HS:
                                scores(g + 1)
                            if g < HS:
                                probabilities(g)
                            if g:
                                values(g - 1)
                            if t and g < HS and h == 2:
                                sums(t - 1)
                            if t and g < HS and h == 5:
                                project_out(t - 1)
                        sums(NT - 1)
                        project_out(NT - 1)

                @block.scalar
                def _(a):
                    a.wait_ge(g_zero, 2)
                    with a.Fori(0, B) as b:
                        a.copy(g_x, Y[:, bass.ds(b, 1), 0:T].rearrange("p a t -> p (a t)")).then_inc(gx_ready, 1)
                        a.wait_ge(gc_ready, done(b))
                        a.copy(g_c, bank(0, 2)).then_inc(gc_out, 1)

                        def out_of(t):
                            for p in (0, 2):
                                a.wait_ge(gT_ready, done(b, 4 * NT, 4 * t + p))
                                a.copy((g_qT, g_kT)[p // 2][:, 0:4, P * t:P * t + P],
                                       bank(4 + p).rearrange("p (c t) -> p c t", c=4)).then_inc(gT_a, 1)

                        for t in range(NT):
                            a.wait_ge(proj_ready, done(b, NT, t))
                            if t >= 2:
                                a.wait_ge(gT_ready, done(b, 4 * NT, 4 * (t - 2) + 3))
                            o = bank(2 * (t % 2))
                            heads = "p (h e) -> p h e"
                            a.copy(g_v[:, t, :, 0:MA_D], o[:, D:2 * D].rearrange(heads, e=MA_D))
                            a.copy(g_k[t % 2][:, :, 0:MA_D], o[:, 0:D].rearrange(heads, e=MA_D)).then_inc(gk_ready, 1)
                            if t:
                                out_of(t - 1)
                        out_of(NT - 1)
                        for g in range(HS + 1):
                            t, h = divmod(g, MA_H)
                            if g < HS:
                                a.wait_ge(gtop_ready, done(b, HS, g))
                                if g >= 2:
                                    a.wait_ge(gt_ready, done(b, len(pieces), number[g - 2, (g - 2) // MA_H // 4]))
                                a.activation(g_p[h % 2][:, 0:P * (t + 1)], bank(2 * (h % 2), 2)[:, 0:P * (t + 1)],
                                             ACT.Exp, bias=g_top[h % 2]).then_inc(gp_ready, 1)
                                for p in range(t // 4 + 1):
                                    n = number[g, p]
                                    if by_a[n]:
                                        piece_out(a, a.copy, b, g, p, n).then_inc(gt_a, 1)
                            if t and h == 0:
                                a.wait_ge(gpv_ready, done(b, HS, g - 1))
                                a.wait_ge(gwo_ready, done(b, NT, t - 2))
                                a.copy(g_o, bank(6)).then_inc(go_out, 1)

                @block.vector
                def _(v):
                    v.wait_ge(w_global, 80)
                    v.wait_ge(g_zero, 2)
                    with v.Fori(0, B) as b:
                        def out_of(t):
                            for p in (1, 3):
                                v.wait_ge(gT_ready, done(b, 4 * NT, 4 * t + p))
                                v.tensor_copy((g_qT, g_kT)[p // 2][:, 4:8, P * t:P * t + P],
                                              bank(4 + p).rearrange("p (c t) -> p c t", c=4)).then_inc(gT_v, 1)

                        for t in range(NT):
                            o = bank(2 * (t % 2) + 1)
                            hr = MA_R // 2
                            v.wait_ge(proj_ready, done(b, NT, t))
                            pair = o[:, 0:2 * MA_R].rearrange("p (a e) -> p a e", e=hr)
                            for r in range(2):
                                last = v.tensor_tensor(
                                    g_rot[t % 2][:, 2 * r:2 * r + 2, :].rearrange("p a (x e) -> p (a x) e", e=hr), pair,
                                    g_tab[:, t, r:r + 1, :].broadcast_to([P, 4, hr]), ALU.mult)
                            last.then_inc(rot_step, 1)
                            v.wait_ge(rot_step, done(b, 2 * NT, 2 * t))
                            c, s, new = g_rot[t % 2][:, 0:2, :], g_rot[t % 2][:, 2:4, :], g_new[t % 2]
                            v.tensor_tensor(new[:, :, 0:hr], c[:, :, 0:hr], s[:, :, hr:MA_R], ALU.subtract)
                            v.tensor_tensor(new[:, :, hr:MA_R], c[:, :, hr:MA_R], s[:, :, 0:hr],
                                            ALU.add).then_inc(rot_step, 1)
                            if t >= 2:
                                v.wait_ge(gT_ready, done(b, 4 * NT, 4 * (t - 2) + 3))
                            v.tensor_scalar(g_q[t % 2][:, :, 0:MA_D],
                                            o[:, 2 * MA_R:D + 2 * MA_R].rearrange("p (h e) -> p h e", e=MA_D),
                                            MA_SCALE, None, ALU.mult)
                            v.wait_ge(rot_step, done(b, 2 * NT, 2 * t + 1))
                            v.tensor_copy(g_k[t % 2][:, :, MA_D:MA_D + MA_R],
                                          new[:, 0:1, :].broadcast_to([P, MA_H, MA_R]))
                            v.tensor_scalar(g_q[t % 2][:, :, MA_D:MA_D + MA_R],
                                            new[:, 1:2, :].broadcast_to([P, MA_H, MA_R]),
                                            MA_SCALE, None, ALU.mult).then_inc(gq_ready, 1)
                            if t:
                                out_of(t - 1)
                        out_of(NT - 1)

                        def top_of(g):
                            t, h = divmod(g, MA_H)
                            v.wait_ge(gs_ready, done(b, HS, g))
                            if g >= 2:
                                v.wait_ge(gp_ready, done(b, HS, g - 2))
                            v.tensor_reduce(g_top[h % 2], bank(2 * (h % 2), 2)[:, 0:P * (t + 1)], AX.X, ALU.max,
                                            negate=True).then_inc(gtop_ready, 1)

                        def over_sums(t):
                            v.wait_ge(gsum_ready, done(b, NT, t))
                            v.reciprocal(g_over, bank(7)).then_inc(gon_step, 1)
                            v.wait_ge(gon_step, done(b, NT, t))
                            v.tensor_tensor(g_on, g_o, g_over, ALU.mult).then_inc(gon_ready, 1)

                        def add(t):
                            v.wait_ge(gwo_ready, done(b, NT, t))
                            x = x_tok[:, bass.ds(b * NT + t, 1), :].rearrange("p a d -> p (a d)")
                            v.tensor_tensor(x, bank(7)[:, 0:P], x, ALU.add).then_inc(gx_added, 1)

                        top_of(0)
                        for g in range(HS):
                            t, h = divmod(g, MA_H)
                            if g + 1 < HS:
                                top_of(g + 1)
                            for p in range(t // 4 + 1):
                                n = number[g, p]
                                if not by_a[n]:
                                    piece_out(v, v.tensor_copy, b, g, p, n).then_inc(gt_v, 1)
                            if t and h == 3:
                                over_sums(t - 1)
                            if t and h == 6:
                                add(t - 1)
                        over_sums(NT - 1)
                        add(NT - 1)

        layer_norm_tokens(True)
        zero_blocks()
        layers(0)
        add_half(0)
        layer_norm_tokens(False)
        global_attention()
        layer_norm_tokens(True)
        zero_blocks()
        layers(1)
        add_half(1)

        with nc.Block() as block:
            @block.sync
            def _(sp):
                sp.dma_start(out.rearrange("b (t p) d -> p (b t) d", p=P), x_tok[:]).then_inc(stored, 16)
                sp.wait_ge(stored, 16)


def window_tables():
    f = np.float32
    half = np.arange(0, DH, 2, dtype=f)
    inv = (f(1.0) / f(10000.0) ** (half / f(DH))).astype(f)
    t = np.arange(T, dtype=f)
    freqs = np.concatenate([t[:, None] * inv[None, :]] * 2, -1).astype(f)
    base = ((half + f(0.4 * DH)) / f(1.4 * DH)).astype(f)
    power = ((t - T // 2) / f(WIN // 2)).astype(f)
    scale = (base[None, :] ** power[:, None]).astype(f)
    scale = np.concatenate([scale, scale], -1)
    cos, sin = np.cos(freqs), np.sin(freqs)
    sin = np.concatenate([-sin[:, :DH // 2], sin[:, DH // 2:]], -1)
    s8 = scale * f(QK_SCALE)
    tab = np.stack([cos * s8, cos / scale, sin * s8, sin / scale], 1).astype(f)
    return np.ascontiguousarray(tab.reshape(NT, P, 4, DH).transpose(1, 0, 2, 3))


def band_mask():
    r = np.arange(P)[:, None] % WIN
    j = np.arange(2 * WIN)[None, :]
    m = np.where((j >= r) & (j <= r + WIN), 0.0, NEG)
    first = np.where((np.arange(P)[:, None] < WIN) & (j < WIN), NEG, m)
    return np.ascontiguousarray(np.stack([first] + [m] * (NT - 1), 1).reshape(P, -1).astype(np.float32))


def square_tables():
    k, m = np.arange(P)[:, None], np.arange(P)[None, :]
    sel = (k == WIN * (m // WIN) + MA_D)
    return np.ascontiguousarray(np.stack(
        [np.eye(P), sel, np.where(m > k, NEG, 0.0)], 1).astype(np.float32))


def global_rotary():
    f = np.float32
    inv = (f(1.0) / f(10000.0) ** (np.arange(0, MA_R, 2, dtype=f) / f(MA_R))).astype(f)
    a = (np.arange(T, dtype=f)[:, None] * inv[None, :]).astype(f)
    tab = np.stack([np.cos(a), np.sin(a)], 1).astype(f)
    return np.ascontiguousarray(tab.reshape(NT, P, 2, MA_R // 2).transpose(1, 0, 2, 3))


def kernel(**inputs):
    import concourse.bacc as bacc
    from concourse.bass_utils import run_bass_kernel_spmd

    g = {k: np.asarray(v) for k, v in inputs.items()}

    def pieces(a, rows):
        n = -(-rows // P)
        pad = np.zeros(a.shape[:-2] + (n * P - rows, a.shape[-1]), a.dtype)
        a = np.concatenate([a, pad], -2)
        return np.moveaxis(a.reshape(a.shape[:-2] + (n, P, a.shape[-1])), -3, -2)

    b1 = g["L0_ffn_b1"]
    cols = [pieces(b1[:, i * F:i * F + F, None], F)[..., 0] for i in range(2)]
    cols += [g[k][:, :, None] for k in ("L0_ffn_ln_g", "L0_ffn_ln_b", "L0_ffn_b2")]
    qs, ks = g["L0_ffn_q_scale"], g["L0_ffn_k_scale"]
    swap = lambda a: np.concatenate([a[:, DH // 2:], a[:, :DH // 2]], -1)
    sc = np.concatenate([qs, ks, swap(qs), swap(ks)], -1)
    ma_o = np.zeros((4, WIN, 4, D), np.float32)
    ma_o[:, :MA_D] = g["L0_attn_W_o"].reshape(4, 4, MA_D, D).transpose(1, 2, 0, 3)
    arrays = {
        "x": g["L0_attn_x"], "wqkv": g["L0_ffn_Wqkv"], "wo": pieces(g["L0_ffn_Wo"], INNER),
        "w1": g["L0_ffn_W1"], "w2": pieces(g["L0_ffn_W2"], F), "vec": np.concatenate(cols, -1),
        "scale": np.repeat(sc[:, None, :], P, 1),
        "ma_down": g["L0_attn_W_kv_down"],
        "ma_up": np.concatenate([g["L0_attn_W_k_up"], g["L0_attn_W_v_up"], g["L0_attn_W_k_rope"]], -1),
        "ma_q": np.concatenate([g["L0_attn_W_q_rope"], g["L0_attn_W_q"]], -1),
        "ma_o": ma_o.reshape(P, 4, D),
        "rotary": window_tables(), "mask": band_mask(), "square": square_tables(),
        "ma_rotary": global_rotary(),
    }
    nc = bacc.Bacc("TRN2", target_bir_lowering=False, num_devices=1)
    laid, args = {}, []
    for name, a in arrays.items():
        laid[f"in_{name}"] = np.ascontiguousarray(a)
        args.append(nc.dram_tensor(f"in_{name}", a.shape, mybir.dt.from_np(a.dtype), kind="ExternalInput").ap())
    args.append(nc.dram_tensor("out_x", (B, T, D), mybir.dt.float32, kind="ExternalOutput").ap())
    macaron_program(nc, *args)
    r = run_bass_kernel_spmd(nc, [laid], core_ids=[0])
    return r.results[0]["out_x"]
```

```python
import concourse.bass as bass
from concourse import mybir
from contextlib import ExitStack
import numpy as np

B, T, D = 2, 1024, 128
P = 128
NT = T // P
DEPTH, HEADS, DH, WIN = 6, 16, 64, 32
INNER = HEADS * DH
PAIRS = HEADS // 2
NW = P // WIN
F = int(D * 4 * 2 / 3)
FP = [min(P, F - P * j) for j in range(-(-F // P))]
NF = len(FP)
UNITS = B * NT
CHUNK = 512
CHUNKS = B * T // CHUNK
QK_SCALE = 8.0
MA_H, MA_D, MA_R = 16, 8, 32
MA_SCALE = float(MA_D + MA_R) ** -0.5
NEG = -3.0e38
CREDIT = 4


def macaron_program(nc, x_in, wqkv_in, wo_in, w1_in, w2_in, vec_in, scale_in, ma_down_in, ma_up_in,
                    ma_q_in, ma_o_in, rotary_in, mask_in, square_in, ma_rotary_in, out):
    fp32, bf16, i32 = mybir.dt.float32, mybir.dt.bfloat16, mybir.dt.int32
    ALU, ACT, AX = mybir.AluOpType, mybir.ActivationFunctionType, mybir.AxisListType
    ctx = ExitStack()
    with ctx:
        def sb(name, shape, dt=fp32):
            return ctx.enter_context(nc.sbuf_tensor(name, shape, dt))

        def sem(name):
            return ctx.enter_context(nc.semaphore(name))

        x_tok = sb("x_tok", [P, B * NT, D])
        X = sb("X", [P, B, T + 4])
        Y = sb("Y", [P, B, T + 4])
        squares = sb("squares", [P, 3, P])
        ident = squares[:, 0, :]
        ident_b = sb("ident_b", [P, P], bf16)
        causal_b = sb("causal_b", [P, 4 * P], bf16)
        band_b = sb("band_b", [P, NT, 2 * WIN], bf16)
        ones = sb("ones", [P, P])
        rotary = sb("rotary", [P, NT, 4, DH])
        mean_w = sb("mean_w", [P, P])
        ln_a = sb("ln_a", [P, B * NT])
        ln_s = [sb(f"ln_s{i}", [P, B * NT]) for i in range(4)]

        pool = sb("pool", [P, 40000])
        at = [0]

        def cut(*shape):
            n = int(np.prod(shape))
            v = pool[:, at[0]:at[0] + n]
            at[0] += n
            names = "abcd"[:len(shape)]
            if len(shape) > 1:
                v = v.rearrange(f"p ({' '.join(names)}) -> p {' '.join(names)}",
                                **dict(zip(names[1:], shape[1:])))
            return v

        wqkv = cut(3 * INNER)
        wo = cut(PAIRS, D)
        w1 = cut(2 * F)
        w2 = cut(NF, D)
        vec = cut(2 * NF + 3)
        scales = cut(4 * DH)
        turn = cut(NT, 4, DH)
        xs = cut(2, P)
        sq = cut(2 * INNER)
        qn = cut(2, HEADS, DH)
        by_cos = cut(2, HEADS, DH)
        rot = cut(2, HEADS, DH)
        ss = cut(2 * HEADS)
        nwt = [cut(2 * HEADS) for _ in range(4)]
        qT = cut(PAIRS, P)
        kT = [cut(PAIRS, 2, WIN + P) for _ in range(2)]
        V = [cut(INNER) for _ in range(4)]
        v_last = [cut(INNER) for _ in range(2)]
        S = cut(HEADS, 2 * WIN)
        top, total, over = cut(HEADS), cut(HEADS), cut(HEADS)
        pT = cut(HEADS, P)
        pT_last = cut(HEADS, WIN)
        turned_P = cut(HEADS, 2 * WIN)
        oT = cut(PAIRS, P)
        kT_end = at[0]
        xc, fsq, xn = cut(CHUNK), cut(CHUNK), cut(CHUNK)
        diag = cut(CHUNK // P, P)
        gel = [cut(CHUNK) for _ in range(2)]
        hid = [cut(CHUNK) for _ in range(NF)]
        var = [cut(CHUNK // P) for _ in range(4)]
        layers_end = at[0]
        at[0] = 0
        ln_x = cut(B * NT, D)
        ln_q = cut(B * NT, D)

        at[0] = 0
        g_x, g_c = cut(T), cut(T)
        g_qT, g_kT = cut(MA_H // 2, T), cut(MA_H // 2, T)
        g_v = cut(NT, MA_H, WIN)
        g_q, g_k = [cut(MA_H, 64) for _ in range(2)], [cut(MA_H, 64) for _ in range(2)]
        g_rot = [cut(4, MA_R) for _ in range(2)]
        g_new = [cut(2, MA_R) for _ in range(2)]
        g_p, g_pT = [cut(T) for _ in range(2)], [cut(T) for _ in range(2)]
        g_top = [cut(1) for _ in range(2)]
        g_o, g_over, g_on = cut(4 * P), cut(4 * P), cut(4 * P)
        g_down, g_up, g_qw, g_wo = cut(D), cut(2 * D + MA_R), cut(D + MA_R), cut(4, D)
        g_tab = cut(NT, 2, MA_R // 2)

        psum = ctx.enter_context(nc.psum_tensor("psum", [P, 4096], fp32))

        def bank(b, n=1):
            return psum[:, 512 * b:512 * (b + n)]

        w_const, w_attn, w_out, w_ffn = sem("w_const"), sem("w_attn"), sem("w_out"), sem("w_ffn")
        kept = [sem("kept0"), sem("kept1")]
        xs_ready, qk_ready, v_ready = sem("xs_ready"), sem("qk_ready"), sem("v_ready")
        sq_ready, qn_ready, cos_ready = sem("sq_ready"), sem("qn_ready"), sem("cos_ready")
        sin_ready, rot_ready, turn_ready = sem("sin_ready"), sem("rot_ready"), sem("turn_ready")
        t_ready, t_out, v_out = sem("t_ready"), sem("t_out"), sem("v_out")
        k_kept, s_ready, s_taken, p_ready = sem("k_kept"), sem("s_ready"), sem("s_taken"), sem("p_ready")
        block_ready, pt_ready = sem("block_ready"), sem("pt_ready")
        o_ready, o_out, wo_ready, y_ready = sem("o_ready"), sem("o_out"), sem("wo_ready"), sem("y_ready")
        norm_step, soft_step = sem("norm_step"), sem("soft_step")
        mu_ready, xc_ready, fsq_ready, var_ready = sem("mu_ready"), sem("xc_ready"), sem("fsq_ready"), sem("var_ready")
        diag_ready, rb_ready, xn_ready = sem("diag_ready"), sem("rb_ready"), sem("xn_ready")
        w1_ready, gel_ready, hid_ready = sem("w1_ready"), sem("gel_ready"), sem("hid_ready")
        w2_ready, x_ready, var_step, aff_step = sem("w2_ready"), sem("x_ready"), sem("var_step"), sem("aff_step")
        set_up, ln_step, ln_ready, ln_T = sem("set_up"), sem("ln_step"), sem("ln_ready"), sem("ln_T")
        flat_ready, flat_T = sem("flat_ready"), sem("flat_T")
        stored = sem("stored")
        gx_ready, gc_ready, gc_out = sem("gx_ready"), sem("gc_ready"), sem("gc_out")
        proj_ready, rot_step, gq_ready = sem("proj_ready"), sem("rot_step"), sem("gq_ready")
        gk_ready, gT_ready, gT_a, gT_v = sem("gk_ready"), sem("gT_ready"), sem("gT_a"), sem("gT_v")
        gs_ready, gtop_ready, gp_ready = sem("gs_ready"), sem("gtop_ready"), sem("gp_ready")
        gt_ready, gt_a, gt_v, gpv_ready = sem("gt_ready"), sem("gt_a"), sem("gt_v"), sem("gpv_ready")
        go_out, gsum_ready, gon_step, gon_ready = sem("go_out"), sem("gsum_ready"), sem("gon_step"), sem("gon_ready")
        gwo_ready, gx_added, w_global, g_zero = sem("gwo_ready"), sem("gx_added"), sem("w_global"), sem("g_zero")
        passed_sp, passed_pool = sem("passed_sp"), sem("passed_pool")

        counted = {
            "tensor": [gc_ready, proj_ready, gT_ready, gs_ready, gt_ready, gpv_ready, gsum_ready, gwo_ready, qk_ready, v_ready, t_ready, s_ready, o_ready, wo_ready, mu_ready, var_ready,
                       rb_ready, w1_ready, w2_ready],
            "scalar": [gx_ready, gc_out, gk_ready, gT_a, gp_ready, gt_a, go_out, xs_ready, sq_ready, v_out, t_out, p_ready, pt_ready, o_out, fsq_ready, gel_ready],
            "vector": [rot_step, gq_ready, gT_v, gtop_ready, gt_v, gon_step, gon_ready, gx_added, qn_ready, cos_ready, s_taken, block_ready, y_ready, norm_step, soft_step,
                       xc_ready, diag_ready, xn_ready, hid_ready, x_ready, var_step, aff_step],
            "gpsimd": [sin_ready, rot_ready, turn_ready, k_kept],
        }

        def done(unit, per=1, part=0):
            return unit * per + part + 1 + CREDIT

        def mean_bank(c):
            return 4 if c else 0

        def var_bank(c):
            return 5 if c else 1

        def spread_bank(c):
            return 4 if c else 2

        def down_bank(c):
            return 5 if c + 1 < CHUNKS else 7

        def kept_by(layer, i, n):
            return (layer * NT + 2 * i + n // 2 + 1) * 16

        def plain(eng):
            eng.sem_inc(passed_sp if eng is nc.sync else passed_pool, 1)

        def rsqrt(v, x, tmp, step, first, op0, c0, op1, c1, between=()):
            u, h, a, y = tmp
            n = [0]
            pieces = iter(between)

            def link(ins):
                ins.then_inc(step, 1)
                n[0] += 1
                for piece in pieces:
                    piece()
                    break
                v.wait_ge(step, first + n[0])

            link(v.tensor_scalar(u, x, c0, c1, op0, op1))
            v.tensor_scalar(h, u, -0.5, None, ALU.mult)
            link(v.tensor_scalar(y.bitcast(i32), u.bitcast(i32), -0.5, 1597463007.0, ALU.mult, ALU.add))
            for _ in range(3):
                link(v.tensor_tensor(a, y, h, ALU.mult))
                link(v.tensor_tensor(a, a, y, ALU.mult))
                link(v.scalar_tensor_tensor(y, a, 1.5, y, ALU.add, ALU.mult))
        RSQRT = 11

        with nc.Block() as block:
            @block.sync
            def _(sp):
                sp.dma_start(x_tok[:], x_in.rearrange("b (t p) d -> p (b t) d", p=P)).then_inc(w_const, 16)
                sp.dma_start(squares[:], square_in).then_inc(w_const, 16)
                sp.dma_start(rotary[:], rotary_in).then_inc(w_const, 16)
                sp.dma_start(pool[:, layers_end:layers_end + NT * 2 * WIN], mask_in).then_inc(w_const, 16)
                sp.wait_ge(w_const, 64)

            @block.vector
            def _(v):
                for s in counted["vector"]:
                    v.sem_inc(s, CREDIT)
                v.wait_ge(w_const, 64)
                v.tensor_copy(ident_b[:], ident)
                v.memset(causal_b[:, 0:3 * P], 0.0)
                v.tensor_copy(causal_b[:, 3 * P:4 * P], squares[:, 2, :])
                v.tensor_copy(band_b[:].rearrange("p t k -> p (t k)"),
                              pool[:, layers_end:layers_end + NT * 2 * WIN]).then_inc(set_up, 1)
                v.memset(ones[:], 1.0)
                v.memset(mean_w[:], 1.0 / D).then_inc(set_up, 1)

            @block.scalar
            def _(a):
                for s in counted["scalar"]:
                    a.sem_inc(s, CREDIT)

            @block.tensor
            def _(pe):
                for s in counted["tensor"]:
                    pe.sem_inc(s, CREDIT)

            @block.gpsimd
            def _(g):
                for s in counted["gpsimd"]:
                    g.sem_inc(s, CREDIT)
                g.memset(X[:], 0.0)
                g.memset(Y[:], 0.0).then_inc(set_up, 1)

        def zero_blocks():
            with nc.Block() as block:
                @block.gpsimd
                def _(g):
                    g.memset(kT[0], 0.0)
                    g.memset(kT[1], 0.0)
                    g.memset(v_last[0], 0.0)
                    g.memset(v_last[1], 0.0).then_inc(set_up, 1)

                @block.vector
                def _(v):
                    v.memset(Y[64:128, :, 0:1], 0.0)
                    v.memset(pT, 0.0)
                    v.memset(pT_last, 0.0)
                    for i in range(4):
                        last = v.memset(V[i], 0.0)
                    last.then_inc(set_up, 1)

        ln_count = [0]

        def layer_norm_tokens(to_skewed):
            r = ln_count[0]
            ln_count[0] += 1
            base = r * (RSQRT + 5)
            with nc.Block() as block:
                @block.vector
                def _(v):
                    n = [base]

                    def link(ins):
                        ins.then_inc(ln_step, 1)
                        n[0] += 1
                        v.wait_ge(ln_step, n[0])

                    wide = [P, B * NT, D]
                    link(v.tensor_reduce(ln_a[:], x_tok[:], AX.X, ALU.add))
                    link(v.tensor_scalar(ln_a[:], ln_a[:], -1.0 / D, None, ALU.mult))
                    link(v.tensor_tensor(ln_x, x_tok[:], ln_a[:].unsqueeze(2).broadcast_to(wide), ALU.add))
                    link(v.tensor_tensor(ln_q, ln_x, ln_x, ALU.mult))
                    link(v.tensor_reduce(ln_a[:], ln_q, AX.X, ALU.add))
                    rsqrt(v, ln_a[:], [t[:] for t in ln_s], ln_step, n[0], ALU.mult, 1.0 / D, ALU.add, 1e-5)
                    v.tensor_tensor(ln_x, ln_x, ln_s[3][:].unsqueeze(2).broadcast_to(wide),
                                    ALU.mult).then_inc(ln_ready, 1)

                @block.tensor
                def _(pe):
                    pe.wait_ge(ln_ready, r + 1)
                    for j in range(B * NT):
                        t = pe.transpose(psum[:, P * j:P * j + P], ln_x[:, j, :], ident)
                        if j % 4 == 3:
                            t.then_inc(ln_T, 1)

                @block.scalar
                def _(a):
                    for j in range(4):
                        a.wait_ge(ln_T, 4 * r + j + 1)
                        b, c = j // 2, CHUNK * (j % 2)
                        if to_skewed:
                            a.copy(X[0:64, b, c:c + CHUNK], bank(j)[0:64, :])
                            a.copy(X[64:128, b, c + 1:c + 1 + CHUNK], bank(j)[64:128, :])
                        else:
                            a.copy(Y[:, b, c:c + CHUNK], bank(j))

        def attention(eng, step):
            for k in range(3):
                step(0, k, lambda d, k=k: k - d >= 0)
            with eng.Fori(0, 3) as i:
                for k in range(3, 7):
                    step(i, k, lambda d: True)
            step(3, 3, lambda d: d >= 0)

        def layers(half):
            with nc.Block() as block:
                L0 = DEPTH * half

                @block.sync
                def _(sp):
                    with sp.Fori(0, DEPTH) as l:
                        U0, C0 = (l + L0) * UNITS, (l + L0) * CHUNKS
                        sp.wait_ge(v_ready, done(U0 - 1))
                        plain(sp)
                        sp.wait_ge(turn_ready, done(l + L0 - 1))
                        plain(sp)
                        sp.dma_start(wqkv, wqkv_in[bass.ds(l, 1)].rearrange("a p n -> p (a n)")).then_inc(w_attn, 16)
                        sp.dma_start(scales, scale_in[bass.ds(l, 1)].rearrange("a p n -> p (a n)")).then_inc(w_attn, 16)
                        sp.wait_ge(wo_ready, done(U0 - 1))
                        plain(sp)
                        sp.dma_start(wo, wo_in[bass.ds(l, 1)].rearrange("a p c n -> p (a c) n")).then_inc(w_out, 16)
                        sp.wait_ge(x_ready, done(C0 - 1))
                        plain(sp)
                        sp.dma_start(w1, w1_in[bass.ds(l, 1)].rearrange("a p n -> p (a n)")).then_inc(w_ffn, 16)
                        sp.dma_start(w2, w2_in[bass.ds(l, 1)].rearrange("a p c n -> p (a c) n")).then_inc(w_ffn, 16)
                        sp.dma_start(vec, vec_in[bass.ds(l, 1)].rearrange("a p n -> p (a n)")).then_inc(w_ffn, 16)

                        def step(i, k, has):
                            U = U0 + 4 * i + k
                            if has(0):
                                sp.wait_ge(o_ready, done(U - 2))
                                sp.wait_ge(v_out, done(U - 2))
                                plain(sp)
                                sp.dma_start(v_last[k % 2][96:128, :],
                                             V[(k - 2) % 4][96:128, :]).then_inc(kept[k % 2], 16)

                        attention(sp, step)

                @block.tensor
                def _(pe):
                    with pe.Fori(0, DEPTH) as l:
                        U0, C0 = (l + L0) * UNITS, (l + L0) * CHUNKS

                        def output(V0, k):
                            pe.wait_ge(o_out, done(V0 + k))
                            for c in range(PAIRS):
                                last = pe.matmul(bank(7)[:, 0:P], wo[:, c, :], oT[:, c, :],
                                                 start=(c == 0), stop=(c == PAIRS - 1))
                            last.then_inc(wo_ready, 1)

                        def turned_scores(V0, i, k, v_behind, between=None):
                            U = V0 + k
                            pe.wait_ge(rot_ready, done(U, 2, 0))
                            if isinstance(i, int) and i == 0 and k == 0:
                                pe.wait_ge(x_ready, done(C0 - 1))
                            for p in range(4):
                                if p == 2:
                                    pe.wait_ge(rot_ready, done(U, 2, 1))
                                if p >= 2:
                                    pe.wait_ge(t_out, done(U, 4, p - 2))
                                for j in range(4):
                                    c = 4 * (p % 2) + j
                                    last = pe.transpose(bank(7 - p % 2)[:, P * j:P * j + P],
                                                        rot[:, p // 2, 2 * c:2 * c + 2, :], ident)
                                last.then_inc(t_ready, 1)
                            if between:
                                between()
                            pe.wait_ge(v_out, done(U + 1 if v_behind else U))
                            if not v_behind:
                                pe.wait_ge(s_taken, done(U - 1))
                            band = band_b[:, bass.ds(2 * i + k // 2, 1), :].broadcast_to([P, HEADS // 2, 2 * WIN])
                            for j in range(2):
                                pe.matmul(bank(4 + j), ident_b[:], band, start=True, stop=False)
                            pe.wait_ge(k_kept, done(U))
                            for c in range(PAIRS):
                                if c % 4 == 0:
                                    pe.wait_ge(t_out, done(U, 4, 2 + c // 4))
                                for w in range(NW):
                                    o = bank(4 + c // 4)[WIN * w:WIN * w + WIN, P * (c % 4):P * (c % 4) + P]
                                    last = pe.matmul(o, qT[:, c, WIN * w:WIN * w + WIN],
                                                     kT[k % 2][:, c, :, WIN * w:WIN * w + 2 * WIN],
                                                     start=False, stop=(c % 4 == 3))
                            last.then_inc(s_ready, 1)

                        def values(V0, i, k):
                            U = V0 + k
                            pe.wait_ge(pt_ready, done(U))
                            pe.wait_ge(y_ready, done(U - 1))
                            pe.wait_ge(kept[k % 2], kept_by(l + L0, i, k))
                            for h in range(HEADS):
                                r = 64 * (h % 2)
                                o = bank(6 + h // 8)[r:r + 64, P * (h // 2 % 4):P * (h // 2 % 4) + P]
                                pe.matmul(o, V[k % 4][:, DH * h:DH * h + DH], pT[:, h, :], start=True, stop=False)
                                last = pe.matmul(o[:, 0:WIN], v_last[k % 2][:, DH * h:DH * h + DH],
                                                 pT_last[:, h, :], start=False, stop=True)
                            last.then_inc(o_ready, 1)

                        def step(i, k, has):
                            U = U0 + 4 * i + k
                            if has(0):
                                if k == 0:
                                    pe.wait_ge(w_attn, (l + L0 + 1) * 32)
                                pe.wait_ge(xs_ready, done(U))
                                pe.wait_ge(qn_ready, done(U - 1))
                                for j in range(4):
                                    last = pe.matmul(bank(j), xs[:, k % 2, :], wqkv[:, 512 * j:512 * j + 512],
                                                     start=True, stop=True)
                                last.then_inc(qk_ready, 1)
                            if has(3):
                                values(U0 + 4 * i, i, k - 3)
                            if has(0):
                                pe.wait_ge(s_taken, done(U - 2))
                                if not has(2):
                                    pe.wait_ge(v_out, done(U - 1))
                                for j in range(2):
                                    last = pe.matmul(bank(4 + j), xs[:, k % 2, :],
                                                     wqkv[:, 2 * INNER + 512 * j:2 * INNER + 512 * j + 512],
                                                     start=True, stop=True)
                                last.then_inc(v_ready, 1)
                            if has(3):
                                pe.wait_ge(o_out, done(U - 3))

                            def behind():
                                if k == 3:
                                    pe.wait_ge(w_out, (l + L0 + 1) * 16)
                                pe.wait_ge(t_out, done(U - 1, 4, 2))
                                output(U0 + 4 * i, k - 3)

                            if has(1):
                                turned_scores(U0 + 4 * i, i, k - 1, has(0), between=behind if has(3) else None)

                        attention(pe, step)

                        def mean(c):
                            pe.wait_ge(y_ready, done(U0 + 2 * (4 * (c // 2) + 3) + c % 2))
                            if c == 0:
                                pe.wait_ge(qn_ready, done(U0 + UNITS - 1))
                            if c == 1:
                                pe.wait_ge(s_taken, done(U0 + UNITS - 1))
                            if c > 1:
                                pe.wait_ge(xn_ready, done(C0 + c - 1))
                            pe.matmul(bank(mean_bank(c)), mean_w[:], Y[:, c % 2, CHUNK * (c // 2):CHUNK * (c // 2) + CHUNK],
                                      start=True, stop=True).then_inc(mu_ready, 1)

                        def variance(c):
                            pe.wait_ge(fsq_ready, done(C0 + c))
                            if c > 1:
                                pe.wait_ge(x_ready, done(C0 + c - 2))
                            for j in range(CHUNK // P):
                                last = pe.matmul(bank(var_bank(c))[:, j:j + 1], fsq[:, P * j:P * j + P], mean_w[:, 0:1],
                                                 start=True, stop=True)
                            last.then_inc(var_ready, 1)

                        def spread(c):
                            pe.wait_ge(diag_ready, done(C0 + c))
                            pe.matmul(bank(spread_bank(c)), ones[:], diag.rearrange("p a b -> p (a b)"),
                                      start=True, stop=True).then_inc(rb_ready, 1)

                        def up(c, j):
                            C = C0 + c
                            if j == 0:
                                pe.wait_ge(xn_ready, done(C))
                            pe.wait_ge(hid_ready, done(C, NF, j - 2))
                            m = FP[j]
                            pe.matmul(bank(2 * (j % 2))[0:m, :], w1[:, P * j:P * j + m], xn, start=True, stop=True)
                            pe.matmul(bank(2 * (j % 2) + 1)[0:m, :], w1[:, F + P * j:F + P * j + m], xn,
                                      start=True, stop=True).then_inc(w1_ready, 1)

                        def down(c):
                            C = C0 + c
                            for j in range(NF):
                                pe.wait_ge(hid_ready, done(C, NF, j))
                                last = pe.matmul(bank(down_bank(c)), w2[0:FP[j], j, :], hid[j][0:FP[j], :],
                                                 start=(j == 0), stop=(j == NF - 1))
                            last.then_inc(w2_ready, 1)

                        W0 = U0 + 12
                        mean(0)
                        values(W0, 3, 1)
                        variance(0)

                        def behind():
                            pe.wait_ge(t_out, done(W0 + 3, 4, 2))
                            output(W0, 1)
                            spread(0)

                        pe.wait_ge(o_out, done(W0 + 1))
                        turned_scores(W0, 3, 3, False, between=behind)
                        values(W0, 3, 2)
                        pe.wait_ge(w_ffn, (l + L0 + 1) * 48)
                        for c in range(CHUNKS):
                            more = c + 1 < CHUNKS
                            if c == 0:
                                up(0, 0)
                                output(W0, 2)
                                mean(1)
                            else:
                                if more:
                                    mean(c + 1)
                                up(c, 0)
                            if c == 1:
                                output(W0, 3)
                            up(c, 1)
                            if more:
                                variance(c + 1)
                            up(c, 2)
                            if more:
                                spread(c + 1)
                            if c == 0:
                                values(W0, 3, 3)
                            down(c)

                @block.scalar
                def _(a):
                    with a.Fori(0, DEPTH) as l:
                        U0, C0 = (l + L0) * UNITS, (l + L0) * CHUNKS

                        def take(i, n):
                            U = U0 + 4 * i + n
                            a.wait_ge(v_ready, done(U - 2))
                            c = n if isinstance(i, int) and 4 * i + n < 2 else CHUNKS - 1
                            a.wait_ge(x_ready, done(C0 - CHUNKS + c))
                            t = 2 * i + n // 2
                            a.copy(xs[:, n % 2, :], X[:, n % 2, bass.ds(t * P, P)]).then_inc(xs_ready, 1)

                        def turned(U, k, parts):
                            a.wait_ge(s_ready, done(U - 1))
                            for p in parts:
                                a.wait_ge(t_ready, done(U, 4, p))
                                if p < 2:
                                    a.copy(qT[:, 4 * p:4 * p + 4, :].rearrange("p c t -> p (c t)"),
                                           bank(7 - p)).then_inc(t_out, 1)
                                    continue
                                if p == 2:
                                    a.wait_ge(k_kept, done(U))
                                c = 4 * (p - 2)
                                for r in range(2):
                                    last = a.copy(kT[k % 2][64 * r:64 * r + 64, c:c + 4, r, WIN:WIN + P],
                                                  bank(7 - p % 2)[64 * r:64 * r + 64, :]
                                                  .rearrange("p (c t) -> p c t", c=4))
                                last.then_inc(t_out, 1)

                        def diagonal(U):
                            a.wait_ge(block_ready, done(U))
                            a.wait_ge(o_ready, done(U - 1))
                            a.copy(pT_last[96:128, :, :], turned_P[0:WIN, :, 0:WIN])
                            for w in range(NW):
                                rows = slice(WIN * w, WIN * w + WIN)
                                if w:
                                    a.copy(pT[WIN * (w - 1):WIN * w, :, rows], turned_P[rows, :, 0:WIN])
                                last = a.copy(pT[rows, :, rows], turned_P[rows, :, WIN:2 * WIN])
                            last.then_inc(pt_ready, 1)

                        def exponents(U):
                            a.wait_ge(s_taken, done(U))
                            a.activation(S, S, ACT.Exp).then_inc(p_ready, 1)

                        def products(U):
                            a.wait_ge(o_ready, done(U))
                            a.wait_ge(wo_ready, done(U - 1))
                            a.copy(oT.rearrange("p c t -> p (c t)"), bank(6, 2)).then_inc(o_out, 1)

                        take(0, 0)

                        def step(i, k, has):
                            U = U0 + 4 * i + k
                            if has(0):
                                a.wait_ge(qk_ready, done(U))
                                a.wait_ge(qn_ready, done(U - 1))
                                a.activation(sq, bank(0, 4), ACT.Square).then_inc(sq_ready, 1)
                            if has(2):
                                exponents(U0 + 4 * i + k - 2)
                            if has(-1):
                                take(i, k + 1)
                            if has(3):
                                products(U0 + 4 * i + k - 3)
                            if has(1):
                                turned(U0 + 4 * i + k - 1, k - 1, (0, 1, 2) if has(3) else ())
                            if has(0):
                                a.wait_ge(v_ready, done(U))
                                a.wait_ge(o_ready, done(U - 4))
                                if k >= 2:
                                    a.wait_ge(kept[k % 2], kept_by(l + L0, i, k - 2))
                                a.copy(V[k % 4], bank(4, 2)).then_inc(v_out, 1)
                            if has(1):
                                turned(U0 + 4 * i + k - 1, k - 1, (3,) if has(3) else range(4))
                            if has(2):
                                diagonal(U0 + 4 * i + k - 2)
                        attention(a, step)

                        def squares_of(c):
                            a.wait_ge(xc_ready, done(C0 + c))
                            a.activation(fsq, xc, ACT.Square).then_inc(fsq_ready, 1)

                        last = U0 + UNITS - 1
                        exponents(last - 1)
                        squares_of(0)
                        products(last - 2)
                        turned(last, UNITS - 1, range(4))
                        diagonal(last - 1)
                        exponents(last)
                        products(last - 1)
                        a.wait_ge(w_ffn, (l + L0 + 1) * 48)
                        for c in range(CHUNKS):
                            if c and c + 1 < CHUNKS:
                                squares_of(c + 1)
                            for j in range(NF):
                                C = C0 + c
                                a.wait_ge(w1_ready, done(C, NF, j))
                                a.wait_ge(hid_ready, done(C, NF, j - 2))
                                m = FP[j]
                                a.activation(gel[j % 2][0:m, :], bank(2 * (j % 2) + 1)[0:m, :], ACT.Gelu,
                                             bias=vec[0:m, NF + j:NF + j + 1]).then_inc(gel_ready, 1)
                                if c == 0 and j == 0:
                                    diagonal(last)
                                    squares_of(1)
                            if c == 0:
                                products(last)

                @block.gpsimd
                def _(g):
                    with g.Fori(0, DEPTH) as l:
                        U0, C0 = (l + L0) * UNITS, (l + L0) * CHUNKS
                        g.wait_ge(w_attn, (l + L0 + 1) * 32)
                        g.wait_ge(cos_ready, done(U0 - 1, 2, 1))
                        g.wait_ge(sin_ready, done(U0 - 1, 2, 1))
                        g.tensor_tensor(turn.rearrange("p t a e -> p t (a e)"),
                                        rotary[:].rearrange("p t a e -> p t (a e)"),
                                        scales.unsqueeze(1).broadcast_to([P, NT, 4 * DH]),
                                        ALU.mult).then_inc(turn_ready, 1)
                        g.wait_ge(turn_ready, done(l + L0))

                        def keep(U, k):
                            g.wait_ge(s_ready, done(U - 2))
                            b = kT[k % 2]
                            plain(g)
                            g.tensor_copy(b[:, :, :, 0:WIN], b[:, :, :, P:P + WIN]).then_inc(k_kept, 1)

                        def step(i, k, has):
                            U = U0 + 4 * i + k
                            if has(1):
                                keep(U - 1, k - 1)
                            if has(0):
                                t = 2 * i + k // 2
                                g.wait_ge(qn_ready, done(U))
                                hd = DH // 2
                                for q in range(2):
                                    g.wait_ge(t_ready, done(U - 1, 4, 2 * q + 1))
                                    plain(g)
                                    for r in range(2):
                                        tab = turn[:, bass.ds(t, 1), 2 + q, hd * r:hd * r + hd].broadcast_to(
                                            [P, HEADS, hd])
                                        last = g.tensor_tensor(rot[:, q, :, hd * r:hd * r + hd],
                                                               qn[:, q, :, hd * (1 - r):hd * (2 - r)], tab, ALU.mult)
                                    last.then_inc(sin_ready, 1)
                                    g.wait_ge(sin_ready, done(U, 2, q))
                                    g.wait_ge(cos_ready, done(U, 2, q))
                                    g.tensor_tensor(rot[:, q], rot[:, q], by_cos[:, q], ALU.add).then_inc(rot_ready, 1)

                        attention(g, step)
                        keep(U0 + UNITS - 1, UNITS - 1)

                @block.vector
                def _(v):
                    with v.Fori(0, DEPTH) as l:
                        U0, C0 = (l + L0) * UNITS, (l + L0) * CHUNKS

                        def probabilities(U):
                            def sums(part):
                                hs = slice(8 * part, 8 * part + 8)
                                if part == 0:
                                    v.wait_ge(p_ready, done(U))
                                v.tensor_reduce(total[:, hs], S[:, hs, :], AX.X, ALU.add).then_inc(soft_step, 1)

                            def over_sums():
                                v.wait_ge(soft_step, done(U, 5, 2))
                                v.reciprocal(over, total).then_inc(soft_step, 1)

                            def normal_part(part):
                                hs = slice(4 * part, 4 * part + 4)
                                if part == 0:
                                    v.wait_ge(soft_step, done(U, 5, 3))
                                ins = v.tensor_tensor(S[:, hs, :], S[:, hs, :], over[:, hs].unsqueeze(2)
                                                      .broadcast_to([P, 4, 2 * WIN]), ALU.mult)
                                if part == 3:
                                    ins.then_inc(soft_step, 1)

                            def turn_part(part):
                                hs = slice(4 * part, 4 * part + 4)
                                if part == 0:
                                    v.wait_ge(soft_step, done(U, 5, 4))
                                    v.wait_ge(pt_ready, done(U - 1))
                                ins = v.transpose(turned_P[:, hs, :], S[:, hs, :])
                                if part == 3:
                                    ins.then_inc(block_ready, 1)

                            return ([lambda: sums(0), lambda: sums(1), over_sums]
                                    + [lambda part=part: normal_part(part) for part in range(4)]
                                    + [lambda part=part: turn_part(part) for part in range(4)])

                        def residual(U, i, k):
                            t, s = 2 * i + k // 2, k % 2
                            v.wait_ge(wo_ready, done(U))
                            v.tensor_tensor(Y[0:64, s, bass.ds(t * P, P)], bank(7)[0:64, 0:P],
                                            X[0:64, s, bass.ds(t * P, P)], ALU.add)
                            v.tensor_tensor(Y[64:128, s, bass.ds(t * P + 1, P)], bank(7)[64:128, 0:P],
                                            X[64:128, s, bass.ds(t * P + 1, P)], ALU.add).then_inc(y_ready, 1)

                        def less_top(U):
                            sc = bank(4, 2).rearrange("p (h e) -> p h e", e=2 * WIN)
                            v.wait_ge(s_ready, done(U))
                            v.tensor_reduce(top, sc, AX.X, ALU.max).then_inc(soft_step, 1)
                            v.wait_ge(soft_step, done(U, 5, 0))
                            v.wait_ge(block_ready, done(U - 1))
                            v.tensor_tensor(S, sc, top.unsqueeze(2).broadcast_to([P, HEADS, 2 * WIN]),
                                            ALU.subtract).then_inc(s_taken, 1)

                        def step(i, k, has):
                            U = U0 + 4 * i + k
                            if has(0):
                                t = 2 * i + k // 2
                                v.wait_ge(sq_ready, done(U))
                                v.tensor_reduce(ss, sq.rearrange("p (h e) -> p h e", e=DH), AX.X,
                                                ALU.add).then_inc(norm_step, 1)
                                v.wait_ge(norm_step, done(U, RSQRT + 1, 0))
                                rsqrt(v, ss, nwt, norm_step, done(U, RSQRT + 1, 0), ALU.max, 1e-24, ALU.mult, 1.0,
                                      between=probabilities(U - 2) if has(2) else ())
                                v.wait_ge(sin_ready, done(U - 1, 2, 1))
                                v.wait_ge(cos_ready, done(U - 1, 2, 1))
                                v.tensor_tensor(qn.rearrange("p q h e -> p (q h) e"),
                                                bank(0, 4).rearrange("p (h e) -> p h e", e=DH),
                                                nwt[3].unsqueeze(2).broadcast_to([P, 2 * HEADS, DH]),
                                                ALU.mult).then_inc(qn_ready, 1)
                                if k == 0:
                                    v.wait_ge(turn_ready, done(l + L0))
                                v.wait_ge(qn_ready, done(U))
                                v.wait_ge(rot_ready, done(U - 1, 2, 1))
                                for q in range(2):
                                    tab = turn[:, bass.ds(t, 1), q, :].broadcast_to([P, HEADS, DH])
                                    v.tensor_tensor(by_cos[:, q], qn[:, q], tab, ALU.mult).then_inc(cos_ready, 1)
                            if has(3):
                                residual(U - 3, i, k - 3)
                            if has(1):
                                less_top(U - 1)

                        attention(v, step)

                        def centre(c):
                            v.wait_ge(mu_ready, done(C0 + c))
                            v.tensor_tensor(xc, Y[:, c % 2, CHUNK * (c // 2):CHUNK * (c // 2) + CHUNK], bank(mean_bank(c)),
                                            ALU.subtract).then_inc(xc_ready, 1)

                        def deviation(c, between=()):
                            v.wait_ge(var_ready, done(C0 + c))
                            rsqrt(v, bank(var_bank(c))[:, 0:CHUNK // P], var, var_step, done(C0 + c, RSQRT, -1),
                                  ALU.mult, 1.0, ALU.add, 1e-5, between=between)
                            for j in range(CHUNK // P):
                                last = v.tensor_scalar(diag[:, j, :], ident, var[3][:, j:j + 1], None, ALU.mult)
                            last.then_inc(diag_ready, 1)

                        def normal(c):
                            v.wait_ge(rb_ready, done(C0 + c))
                            v.tensor_tensor(xn, xc, bank(spread_bank(c)), ALU.mult).then_inc(aff_step, 1)
                            v.wait_ge(aff_step, done(C0 + c))
                            v.tensor_scalar(xn, xn, vec[:, 2 * NF:2 * NF + 1], vec[:, 2 * NF + 1:2 * NF + 2],
                                            ALU.mult, ALU.add).then_inc(xn_ready, 1)

                        def hidden(c, j):
                            m = FP[j]
                            v.wait_ge(gel_ready, done(C0 + c, NF, j))
                            v.wait_ge(w2_ready, done(C0 + c - 1))
                            v.scalar_tensor_tensor(hid[j][0:m, :], bank(2 * (j % 2))[0:m, :], vec[0:m, j:j + 1],
                                                   gel[j % 2][0:m, :], ALU.add, ALU.mult).then_inc(hid_ready, 1)

                        def result(c):
                            b, at0 = c % 2, CHUNK * (c // 2)
                            v.wait_ge(w2_ready, done(C0 + c))
                            for r in range(2):
                                rows = slice(64 * r, 64 * r + 64)
                                last = v.scalar_tensor_tensor(
                                    X[rows, b, at0 + r:at0 + r + CHUNK], bank(down_bank(c))[rows, :],
                                    vec[rows, 2 * NF + 2:2 * NF + 3], Y[rows, b, at0 + r:at0 + r + CHUNK],
                                    ALU.add, ALU.add)
                            last.then_inc(x_ready, 1)

                        W0 = U0 + 12
                        centre(0)
                        deviation(0, between=probabilities(W0 + 2))
                        residual(W0 + 1, 3, 1)
                        v.wait_ge(w_ffn, (l + L0 + 1) * 48)
                        normal(0)
                        less_top(W0 + 3)
                        for piece in probabilities(W0 + 3):
                            piece()
                        residual(W0 + 2, 3, 2)
                        for c in range(CHUNKS):
                            more = c + 1 < CHUNKS
                            if c and more:
                                centre(c + 1)
                            hidden(c, 0)
                            if c == 0:
                                centre(1)
                            if c == 1:
                                residual(W0 + 3, 3, 3)
                            if more and c:
                                deviation(c + 1)
                            hidden(c, 1)
                            if c == 0:
                                deviation(1)
                            hidden(c, 2)
                            if more:
                                normal(c + 1)
                            result(c)

        def add_half(half):
            with nc.Block() as block:
                @block.scalar
                def _(a):
                    for b in range(B):
                        a.copy(Y[0:64, b, 0:T], X[0:64, b, 0:T])
                        a.copy(Y[64:128, b, 0:T], X[64:128, b, 1:T + 1]).then_inc(flat_ready, 1)

                @block.tensor
                def _(pe):
                    for j in range(B * NT):
                        if j % NT == 0:
                            pe.wait_ge(flat_ready, B * half + j // NT + 1)
                        t = pe.transpose(psum[:, P * j:P * j + P], Y[:, j // NT, P * (j % NT):P * (j % NT) + P], ident)
                        if j % 4 == 3:
                            t.then_inc(flat_T, 1)

                @block.vector
                def _(v):
                    for j in range(4):
                        v.wait_ge(flat_T, 4 * half + j + 1)
                        x = x_tok[:, 4 * j:4 * j + 4, :].rearrange("p a d -> p (a d)")
                        v.scalar_tensor_tensor(x, bank(j), 0.5, x, ALU.mult, ALU.add)

        def global_attention():
            HS = NT * MA_H
            pieces = [(g, p) for g in range(HS) for p in range(g // MA_H // 4 + 1)]
            number = {gp: n for n, gp in enumerate(pieces)}
            by_a = [n % 2 == 0 for n in range(len(pieces))]

            def moved(b, n):
                own = [m for m in range(len(pieces)) if by_a[m] == by_a[n]]
                return (gt_a if by_a[n] else gt_v), done(b, len(own), own.index(n))

            def piece_out(eng, copy, b, g, p, n):
                t, h = divmod(g, MA_H)
                eng.wait_ge(gt_ready, done(b, len(pieces), n))
                if g >= 2:
                    eng.wait_ge(gpv_ready, done(b, HS, g - 2))
                m = P * min(4, t + 1 - 4 * p)
                return copy(g_pT[h % 2][:, 512 * p:512 * p + m], bank(4 + p)[:, 0:m])

            with nc.Block() as block:
                @block.sync
                def _(sp):
                    for a, b in ((g_down, ma_down_in), (g_up, ma_up_in), (g_qw, ma_q_in), (g_wo, ma_o_in),
                                 (g_tab, ma_rotary_in)):
                        sp.dma_start(a, b).then_inc(w_global, 16)

                @block.gpsimd
                def _(g):
                    for i in range(2):
                        g.memset(g_q[i], 0.0)
                        g.memset(g_k[i], 0.0)
                    g.memset(g_v, 0.0).then_inc(g_zero, 1)
                    g.wait_ge(g_zero, 1)
                    g.memset(g_v[:, :, :, MA_D:MA_D + 1], 1.0).then_inc(g_zero, 1)

                @block.tensor
                def _(pe):
                    pe.wait_ge(w_global, 80)
                    with pe.Fori(0, B) as b:
                        pe.wait_ge(gx_ready, done(b))
                        for j in range(2):
                            last = pe.matmul(bank(j), g_down, g_x[:, 512 * j:512 * j + 512], start=True, stop=True)
                        last.then_inc(gc_ready, 1)
                        pe.wait_ge(gc_out, done(b))

                        def project(t):
                            o, o2 = bank(2 * (t % 2)), bank(2 * (t % 2) + 1)
                            if t >= 2:
                                pe.wait_ge(gq_ready, done(b, NT, t - 2))
                                pe.wait_ge(gk_ready, done(b, NT, t - 2))
                            c = slice(P * t, P * t + P)
                            pe.matmul(o[:, 0:2 * D], g_c[:, c], g_up[:, 0:2 * D], start=True, stop=True)
                            pe.matmul(o2[:, 0:MA_R], g_c[:, c], g_up[:, 2 * D:2 * D + MA_R], start=True, stop=True)
                            pe.matmul(o2[:, MA_R:D + 2 * MA_R], g_x[:, c], g_qw,
                                      start=True, stop=True).then_inc(proj_ready, 1)

                        def turn_over(t):
                            pe.wait_ge(gq_ready, done(b, NT, t))
                            pe.wait_ge(gk_ready, done(b, NT, t))
                            for p in range(4):
                                if t:
                                    pe.wait_ge((gT_a, gT_v)[p % 2], done(b, 2 * NT, 2 * (t - 1) + p // 2))
                                for j in range(4):
                                    c = 4 * (p % 2) + j
                                    last = pe.transpose(bank(4 + p)[:, P * j:P * j + P],
                                                        (g_q, g_k)[p // 2][t % 2][:, 2 * c:2 * c + 2, :], ident)
                                last.then_inc(gT_ready, 1)

                        project(0)
                        for t in range(NT):
                            if t + 1 < NT:
                                project(t + 1)
                            turn_over(t)
                        pe.wait_ge(gT_a, done(b, 2 * NT, 2 * NT - 1))
                        pe.wait_ge(gT_v, done(b, 2 * NT, 2 * NT - 1))

                        def scores(g):
                            t, h = divmod(g, MA_H)
                            if g >= 2:
                                pe.wait_ge(gp_ready, done(b, HS, g - 2))
                            r, c = 64 * (h % 2), h // 2
                            q = g_qT[r:r + 64, c, P * t:P * t + P]
                            for j in range(t // 4 + 1):
                                n = min(P * (t + 1) - 512 * j, 512)
                                o = bank(2 * (h % 2) + j)
                                diagonal = 512 * j <= P * t < 512 * j + n
                                if diagonal:
                                    pe.matmul(o[:, 0:n], ident_b[:], causal_b[:, 512 - n:512],
                                              start=True, stop=False)
                                last = pe.matmul(o[:, 0:n], q, g_kT[r:r + 64, c, 512 * j:512 * j + n],
                                                 start=not diagonal, stop=True)
                            last.then_inc(gs_ready, 1)

                        def probabilities(g):
                            t, h = divmod(g, MA_H)
                            pe.wait_ge(gp_ready, done(b, HS, g))
                            for p in range(t // 4 + 1):
                                if (g - 1, p) in number:
                                    pe.wait_ge(*moved(b, number[g - 1, p]))
                                for j in range(min(4, t + 1 - 4 * p)):
                                    k = 4 * p + j
                                    last = pe.transpose(bank(4 + p)[:, P * j:P * j + P],
                                                        g_p[h % 2][:, P * k:P * k + P], ident)
                                last.then_inc(gt_ready, 1)

                        def values(g):
                            t, h = divmod(g, MA_H)
                            for p in range(t // 4 + 1):
                                pe.wait_ge(*moved(b, number[g, p]))
                            if h == 0 and t:
                                pe.wait_ge(go_out, done(b, NT, t - 1))
                            for k in range(t + 1):
                                last = pe.matmul(bank(6)[WIN * (h % 4):WIN * (h % 4) + WIN, P * (h // 4):P * (h // 4) + P],
                                                 g_v[:, k, h, :], g_pT[h % 2][:, P * k:P * k + P],
                                                 start=(k == 0), stop=(k == t))
                            last.then_inc(gpv_ready, 1)

                        def sums(t):
                            pe.wait_ge(go_out, done(b, NT, t))
                            if t:
                                pe.wait_ge(gx_added, done(b, NT, t - 1))
                            pe.matmul(bank(7), squares[:, 1, :], g_o, start=True, stop=True).then_inc(gsum_ready, 1)

                        def project_out(t):
                            pe.wait_ge(gon_ready, done(b, NT, t))
                            for j in range(4):
                                last = pe.matmul(bank(7)[:, 0:P], g_on[:, P * j:P * j + P], g_wo[:, j, :],
                                                 start=(j == 0), stop=(j == 3))
                            last.then_inc(gwo_ready, 1)

                        scores(0)
                        for g in range(HS + 1):
                            t, h = divmod(g, MA_H)
                            if g + 1 < HS:
                                scores(g + 1)
                            if g < HS:
                                probabilities(g)
                            if g:
                                values(g - 1)
                            if t and g < HS and h == 2:
                                sums(t - 1)
                            if t and g < HS and h == 5:
                                project_out(t - 1)
                        sums(NT - 1)
                        project_out(NT - 1)

                @block.scalar
                def _(a):
                    a.wait_ge(g_zero, 2)
                    with a.Fori(0, B) as b:
                        a.copy(g_x, Y[:, bass.ds(b, 1), 0:T].rearrange("p a t -> p (a t)")).then_inc(gx_ready, 1)
                        a.wait_ge(gc_ready, done(b))
                        a.copy(g_c, bank(0, 2)).then_inc(gc_out, 1)

                        def out_of(t):
                            for p in (0, 2):
                                a.wait_ge(gT_ready, done(b, 4 * NT, 4 * t + p))
                                a.copy((g_qT, g_kT)[p // 2][:, 0:4, P * t:P * t + P],
                                       bank(4 + p).rearrange("p (c t) -> p c t", c=4)).then_inc(gT_a, 1)

                        for t in range(NT):
                            a.wait_ge(proj_ready, done(b, NT, t))
                            if t >= 2:
                                a.wait_ge(gT_ready, done(b, 4 * NT, 4 * (t - 2) + 3))
                            o = bank(2 * (t % 2))
                            heads = "p (h e) -> p h e"
                            a.copy(g_v[:, t, :, 0:MA_D], o[:, D:2 * D].rearrange(heads, e=MA_D))
                            a.copy(g_k[t % 2][:, :, 0:MA_D], o[:, 0:D].rearrange(heads, e=MA_D)).then_inc(gk_ready, 1)
                            if t:
                                out_of(t - 1)
                        out_of(NT - 1)
                        for g in range(HS + 1):
                            t, h = divmod(g, MA_H)
                            if g < HS:
                                a.wait_ge(gtop_ready, done(b, HS, g))
                                if g >= 2:
                                    a.wait_ge(gt_ready, done(b, len(pieces), number[g - 2, (g - 2) // MA_H // 4]))
                                a.activation(g_p[h % 2][:, 0:P * (t + 1)], bank(2 * (h % 2), 2)[:, 0:P * (t + 1)],
                                             ACT.Exp, bias=g_top[h % 2]).then_inc(gp_ready, 1)
                                for p in range(t // 4 + 1):
                                    n = number[g, p]
                                    if by_a[n]:
                                        piece_out(a, a.copy, b, g, p, n).then_inc(gt_a, 1)
                            if t and h == 0:
                                a.wait_ge(gpv_ready, done(b, HS, g - 1))
                                a.wait_ge(gwo_ready, done(b, NT, t - 2))
                                a.copy(g_o, bank(6)).then_inc(go_out, 1)

                @block.vector
                def _(v):
                    v.wait_ge(w_global, 80)
                    v.wait_ge(g_zero, 2)
                    with v.Fori(0, B) as b:
                        def out_of(t):
                            for p in (1, 3):
                                v.wait_ge(gT_ready, done(b, 4 * NT, 4 * t + p))
                                v.tensor_copy((g_qT, g_kT)[p // 2][:, 4:8, P * t:P * t + P],
                                              bank(4 + p).rearrange("p (c t) -> p c t", c=4)).then_inc(gT_v, 1)

                        for t in range(NT):
                            o = bank(2 * (t % 2) + 1)
                            hr = MA_R // 2
                            v.wait_ge(proj_ready, done(b, NT, t))
                            pair = o[:, 0:2 * MA_R].rearrange("p (a e) -> p a e", e=hr)
                            for r in range(2):
                                last = v.tensor_tensor(
                                    g_rot[t % 2][:, 2 * r:2 * r + 2, :].rearrange("p a (x e) -> p (a x) e", e=hr), pair,
                                    g_tab[:, t, r:r + 1, :].broadcast_to([P, 4, hr]), ALU.mult)
                            last.then_inc(rot_step, 1)
                            v.wait_ge(rot_step, done(b, 2 * NT, 2 * t))
                            c, s, new = g_rot[t % 2][:, 0:2, :], g_rot[t % 2][:, 2:4, :], g_new[t % 2]
                            v.tensor_tensor(new[:, :, 0:hr], c[:, :, 0:hr], s[:, :, hr:MA_R], ALU.subtract)
                            v.tensor_tensor(new[:, :, hr:MA_R], c[:, :, hr:MA_R], s[:, :, 0:hr],
                                            ALU.add).then_inc(rot_step, 1)
                            if t >= 2:
                                v.wait_ge(gT_ready, done(b, 4 * NT, 4 * (t - 2) + 3))
                            v.tensor_scalar(g_q[t % 2][:, :, 0:MA_D],
                                            o[:, 2 * MA_R:D + 2 * MA_R].rearrange("p (h e) -> p h e", e=MA_D),
                                            MA_SCALE, None, ALU.mult)
                            v.wait_ge(rot_step, done(b, 2 * NT, 2 * t + 1))
                            v.tensor_copy(g_k[t % 2][:, :, MA_D:MA_D + MA_R],
                                          new[:, 0:1, :].broadcast_to([P, MA_H, MA_R]))
                            v.tensor_scalar(g_q[t % 2][:, :, MA_D:MA_D + MA_R],
                                            new[:, 1:2, :].broadcast_to([P, MA_H, MA_R]),
                                            MA_SCALE, None, ALU.mult).then_inc(gq_ready, 1)
                            if t:
                                out_of(t - 1)
                        out_of(NT - 1)

                        def top_of(g):
                            t, h = divmod(g, MA_H)
                            v.wait_ge(gs_ready, done(b, HS, g))
                            if g >= 2:
                                v.wait_ge(gp_ready, done(b, HS, g - 2))
                            v.tensor_reduce(g_top[h % 2], bank(2 * (h % 2), 2)[:, 0:P * (t + 1)], AX.X, ALU.max,
                                            negate=True).then_inc(gtop_ready, 1)

                        def over_sums(t):
                            v.wait_ge(gsum_ready, done(b, NT, t))
                            v.reciprocal(g_over, bank(7)).then_inc(gon_step, 1)
                            v.wait_ge(gon_step, done(b, NT, t))
                            v.tensor_tensor(g_on, g_o, g_over, ALU.mult).then_inc(gon_ready, 1)

                        def add(t):
                            v.wait_ge(gwo_ready, done(b, NT, t))
                            x = x_tok[:, bass.ds(b * NT + t, 1), :].rearrange("p a d -> p (a d)")
                            v.tensor_tensor(x, bank(7)[:, 0:P], x, ALU.add).then_inc(gx_added, 1)

                        top_of(0)
                        for g in range(HS):
                            t, h = divmod(g, MA_H)
                            if g + 1 < HS:
                                top_of(g + 1)
                            for p in range(t // 4 + 1):
                                n = number[g, p]
                                if not by_a[n]:
                                    piece_out(v, v.tensor_copy, b, g, p, n).then_inc(gt_v, 1)
                            if t and h == 3:
                                over_sums(t - 1)
                            if t and h == 6:
                                add(t - 1)
                        over_sums(NT - 1)
                        add(NT - 1)

        layer_norm_tokens(True)
        zero_blocks()
        layers(0)
        add_half(0)
        layer_norm_tokens(False)
        global_attention()
        layer_norm_tokens(True)
        zero_blocks()
        layers(1)
        add_half(1)

        with nc.Block() as block:
            @block.sync
            def _(sp):
                sp.dma_start(out.rearrange("b (t p) d -> p (b t) d", p=P), x_tok[:]).then_inc(stored, 16)
                sp.wait_ge(stored, 16)


def window_tables():
    f = np.float32
    half = np.arange(0, DH, 2, dtype=f)
    inv = (f(1.0) / f(10000.0) ** (half / f(DH))).astype(f)
    t = np.arange(T, dtype=f)
    freqs = np.concatenate([t[:, None] * inv[None, :]] * 2, -1).astype(f)
    base = ((half + f(0.4 * DH)) / f(1.4 * DH)).astype(f)
    power = ((t - T // 2) / f(WIN // 2)).astype(f)
    scale = (base[None, :] ** power[:, None]).astype(f)
    scale = np.concatenate([scale, scale], -1)
    cos, sin = np.cos(freqs), np.sin(freqs)
    sin = np.concatenate([-sin[:, :DH // 2], sin[:, DH // 2:]], -1)
    s8 = scale * f(QK_SCALE)
    tab = np.stack([cos * s8, cos / scale, sin * s8, sin / scale], 1).astype(f)
    return np.ascontiguousarray(tab.reshape(NT, P, 4, DH).transpose(1, 0, 2, 3))


def band_mask():
    r = np.arange(P)[:, None] % WIN
    j = np.arange(2 * WIN)[None, :]
    m = np.where((j >= r) & (j <= r + WIN), 0.0, NEG)
    first = np.where((np.arange(P)[:, None] < WIN) & (j < WIN), NEG, m)
    return np.ascontiguousarray(np.stack([first] + [m] * (NT - 1), 1).reshape(P, -1).astype(np.float32))


def square_tables():
    k, m = np.arange(P)[:, None], np.arange(P)[None, :]
    sel = (k == WIN * (m // WIN) + MA_D)
    return np.ascontiguousarray(np.stack(
        [np.eye(P), sel, np.where(m > k, NEG, 0.0)], 1).astype(np.float32))


def global_rotary():
    f = np.float32
    inv = (f(1.0) / f(10000.0) ** (np.arange(0, MA_R, 2, dtype=f) / f(MA_R))).astype(f)
    a = (np.arange(T, dtype=f)[:, None] * inv[None, :]).astype(f)
    tab = np.stack([np.cos(a), np.sin(a)], 1).astype(f)
    return np.ascontiguousarray(tab.reshape(NT, P, 2, MA_R // 2).transpose(1, 0, 2, 3))


def kernel(**inputs):
    import concourse.bacc as bacc
    from concourse.bass_utils import run_bass_kernel_spmd

    g = {k: np.asarray(v) for k, v in inputs.items()}

    def pieces(a, rows):
        n = -(-rows // P)
        pad = np.zeros(a.shape[:-2] + (n * P - rows, a.shape[-1]), a.dtype)
        a = np.concatenate([a, pad], -2)
        return np.moveaxis(a.reshape(a.shape[:-2] + (n, P, a.shape[-1])), -3, -2)

    b1 = g["L0_ffn_b1"]
    cols = [pieces(b1[:, i * F:i * F + F, None], F)[..., 0] for i in range(2)]
    cols += [g[k][:, :, None] for k in ("L0_ffn_ln_g", "L0_ffn_ln_b", "L0_ffn_b2")]
    qs, ks = g["L0_ffn_q_scale"], g["L0_ffn_k_scale"]
    swap = lambda a: np.concatenate([a[:, DH // 2:], a[:, :DH // 2]], -1)
    sc = np.concatenate([qs, ks, swap(qs), swap(ks)], -1)
    ma_o = np.zeros((4, WIN, 4, D), np.float32)
    ma_o[:, :MA_D] = g["L0_attn_W_o"].reshape(4, 4, MA_D, D).transpose(1, 2, 0, 3)
    arrays = {
        "x": g["L0_attn_x"], "wqkv": g["L0_ffn_Wqkv"], "wo": pieces(g["L0_ffn_Wo"], INNER),
        "w1": g["L0_ffn_W1"], "w2": pieces(g["L0_ffn_W2"], F), "vec": np.concatenate(cols, -1),
        "scale": np.repeat(sc[:, None, :], P, 1),
        "ma_down": g["L0_attn_W_kv_down"],
        "ma_up": np.concatenate([g["L0_attn_W_k_up"], g["L0_attn_W_v_up"], g["L0_attn_W_k_rope"]], -1),
        "ma_q": np.concatenate([g["L0_attn_W_q_rope"], g["L0_attn_W_q"]], -1),
        "ma_o": ma_o.reshape(P, 4, D),
        "rotary": window_tables(), "mask": band_mask(), "square": square_tables(),
        "ma_rotary": global_rotary(),
    }
    nc = bacc.Bacc("TRN2", target_bir_lowering=False, num_devices=1)
    laid, args = {}, []
    for name, a in arrays.items():
        laid[f"in_{name}"] = np.ascontiguousarray(a)
        args.append(nc.dram_tensor(f"in_{name}", a.shape, mybir.dt.from_np(a.dtype), kind="ExternalInput").ap())
    args.append(nc.dram_tensor("out_x", (B, T, D), mybir.dt.float32, kind="ExternalOutput").ap())
    macaron_program(nc, *args)
    r = run_bass_kernel_spmd(nc, [laid], core_ids=[0])
    return r.results[0]["out_x"]
```

```python
import concourse.bass as bass
from concourse import mybir
from contextlib import ExitStack
import numpy as np

B, T, D = 2, 1024, 128
P = 128
NT = T // P
DEPTH, HEADS, DH, WIN = 6, 16, 64, 32
INNER = HEADS * DH
PAIRS = HEADS // 2
NW = P // WIN
F = int(D * 4 * 2 / 3)
FP = [min(P, F - P * j) for j in range(-(-F // P))]
NF = len(FP)
UNITS = B * NT
CHUNK = 512
CHUNKS = B * T // CHUNK
QK_SCALE = 8.0
MA_H, MA_D, MA_R = 16, 8, 32
MA_SCALE = float(MA_D + MA_R) ** -0.5
NEG = -3.0e38
CREDIT = 4


def macaron_program(nc, x_in, wqkv_in, wo_in, w1_in, w2_in, vec_in, scale_in, ma_down_in, ma_up_in,
                    ma_q_in, ma_o_in, rotary_in, mask_in, square_in, ma_rotary_in, out):
    fp32, bf16, i32, f32r = mybir.dt.float32, mybir.dt.bfloat16, mybir.dt.int32, mybir.dt.float32r
    ALU, ACT, AX = mybir.AluOpType, mybir.ActivationFunctionType, mybir.AxisListType
    ctx = ExitStack()
    with ctx:
        def sb(name, shape, dt=fp32):
            return ctx.enter_context(nc.sbuf_tensor(name, shape, dt))

        def sem(name):
            return ctx.enter_context(nc.semaphore(name))

        x_tok = sb("x_tok", [P, B * NT, D])
        X = sb("X", [P, B, T + 4])
        Y = sb("Y", [P, B, T + 4])
        squares = sb("squares", [P, 3, P])
        ident = squares[:, 0, :]
        ident_b = sb("ident_b", [P, P], bf16)
        causal_b = sb("causal_b", [P, 4 * P], bf16)
        band_b = sb("band_b", [P, NT, 2 * WIN], bf16)
        ones = sb("ones", [P, P])
        rotary = sb("rotary", [P, NT, 4, DH])
        mean_w = sb("mean_w", [P, P])
        ln_a = sb("ln_a", [P, B * NT])
        ln_s = [sb(f"ln_s{i}", [P, B * NT]) for i in range(4)]

        wqkv_hi, wqkv_lo = sb("wqkv_hi", [P, 3 * INNER], f32r), sb("wqkv_lo", [P, 3 * INNER], f32r)
        xs_hi, xs_lo = sb("xs_hi", [P, 2, P], f32r), sb("xs_lo", [P, 2, P], f32r)

        pool = sb("pool", [P, 36200])
        at = [0]

        def cut(*shape):
            n = int(np.prod(shape))
            v = pool[:, at[0]:at[0] + n]
            at[0] += n
            names = "abcd"[:len(shape)]
            if len(shape) > 1:
                v = v.rearrange(f"p ({' '.join(names)}) -> p {' '.join(names)}",
                                **dict(zip(names[1:], shape[1:])))
            return v

        wo = cut(PAIRS, D)
        w1 = cut(2 * F)
        w2 = cut(NF, D)
        vec = cut(2 * NF + 3)
        scales = cut(4 * DH)
        turn = cut(NT, 4, DH)
        xs = cut(2, P)
        wqkv = pool[:, at[0]:at[0] + 3 * INNER]
        sq = cut(2 * INNER)
        qn = cut(2, HEADS, DH)
        by_cos = cut(2, HEADS, DH)
        rot = cut(2, HEADS, DH)
        ss = cut(2 * HEADS)
        nwt = [cut(2 * HEADS) for _ in range(4)]
        qT = cut(PAIRS, P)
        kT = [cut(PAIRS, 2, WIN + P) for _ in range(2)]
        V = [cut(INNER) for _ in range(4)]
        v_last = [cut(INNER) for _ in range(2)]
        S = cut(HEADS, 2 * WIN)
        top, total, over = cut(HEADS), cut(HEADS), cut(HEADS)
        pT = cut(HEADS, P)
        pT_last = cut(HEADS, WIN)
        turned_P = cut(HEADS, 2 * WIN)
        oT = cut(PAIRS, P)
        kT_end = at[0]
        xc, fsq, xn = cut(CHUNK), cut(CHUNK), cut(CHUNK)
        diag = cut(CHUNK // P, P)
        gel = [cut(CHUNK) for _ in range(2)]
        hid = [cut(CHUNK) for _ in range(NF)]
        var = [cut(CHUNK // P) for _ in range(4)]
        layers_end = at[0]
        ln_parts = []
        for start in (0, kT_end):
            at[0] = start
            ln_parts.append((cut(B * NT, D), cut(B * NT, D)))

        at[0] = 0
        g_x, g_c = cut(T), cut(T)
        g_qT, g_kT = cut(MA_H // 2, T), cut(MA_H // 2, T)
        g_v = cut(NT, MA_H, WIN)
        g_q, g_k = [cut(MA_H, 64) for _ in range(2)], [cut(MA_H, 64) for _ in range(2)]
        g_rot = [cut(4, MA_R) for _ in range(2)]
        g_new = [cut(2, MA_R) for _ in range(2)]
        g_p, g_pT = [cut(T) for _ in range(2)], [cut(T) for _ in range(2)]
        g_top = [cut(1) for _ in range(2)]
        g_o, g_over, g_on = cut(4 * P), cut(4 * P), cut(4 * P)
        g_down, g_up, g_qw, g_wo = cut(D), cut(2 * D + MA_R), cut(D + MA_R), cut(4, D)
        g_tab = cut(NT, 2, MA_R // 2)

        psum = ctx.enter_context(nc.psum_tensor("psum", [P, 4096], fp32))

        def bank(b, n=1):
            return psum[:, 512 * b:512 * (b + n)]

        w_const, w_attn, w_out, w_ffn = sem("w_const"), sem("w_attn"), sem("w_out"), sem("w_ffn")
        kept = [sem("kept0"), sem("kept1")]
        xs_ready, qk_ready, v_ready = sem("xs_ready"), sem("qk_ready"), sem("v_ready")
        lo_ready, w_hi, w_split = sem("lo_ready"), sem("w_hi"), sem("w_split")
        sq_ready, qn_ready, cos_ready = sem("sq_ready"), sem("qn_ready"), sem("cos_ready")
        sin_ready, rot_ready, turn_ready = sem("sin_ready"), sem("rot_ready"), sem("turn_ready")
        t_ready, t_out, v_out = sem("t_ready"), sem("t_out"), sem("v_out")
        k_kept, s_ready, s_taken, p_ready = sem("k_kept"), sem("s_ready"), sem("s_taken"), sem("p_ready")
        block_ready, pt_ready = sem("block_ready"), sem("pt_ready")
        o_ready, o_out, wo_ready, y_ready = sem("o_ready"), sem("o_out"), sem("wo_ready"), sem("y_ready")
        norm_step, soft_step = sem("norm_step"), sem("soft_step")
        mu_ready, xc_ready, fsq_ready, var_ready = sem("mu_ready"), sem("xc_ready"), sem("fsq_ready"), sem("var_ready")
        diag_ready, rb_ready, xn_ready = sem("diag_ready"), sem("rb_ready"), sem("xn_ready")
        w1_ready, gel_ready, hid_ready = sem("w1_ready"), sem("gel_ready"), sem("hid_ready")
        w2_ready, x_ready, var_step, aff_step = sem("w2_ready"), sem("x_ready"), sem("var_step"), sem("aff_step")
        set_up, ln_step, ln_ready, ln_T = sem("set_up"), sem("ln_step"), sem("ln_ready"), sem("ln_T")
        flat_ready, flat_T = sem("flat_ready"), sem("flat_T")
        stored = sem("stored")
        gx_ready, gc_ready, gc_out = sem("gx_ready"), sem("gc_ready"), sem("gc_out")
        proj_ready, rot_step, gq_ready = sem("proj_ready"), sem("rot_step"), sem("gq_ready")
        gk_ready, gT_ready, gT_a, gT_v = sem("gk_ready"), sem("gT_ready"), sem("gT_a"), sem("gT_v")
        gs_ready, gtop_ready, gp_ready = sem("gs_ready"), sem("gtop_ready"), sem("gp_ready")
        gt_ready, gt_a, gt_v, gpv_ready = sem("gt_ready"), sem("gt_a"), sem("gt_v"), sem("gpv_ready")
        go_out, gsum_ready, gon_step, gon_ready = sem("go_out"), sem("gsum_ready"), sem("gon_step"), sem("gon_ready")
        gwo_ready, gx_added, w_global, g_zero = sem("gwo_ready"), sem("gx_added"), sem("w_global"), sem("g_zero")
        passed_sp, passed_pool = sem("passed_sp"), sem("passed_pool")

        counted = {
            "tensor": [gc_ready, proj_ready, gT_ready, gs_ready, gt_ready, gpv_ready, gsum_ready, gwo_ready, qk_ready, v_ready, t_ready, s_ready, o_ready, wo_ready, mu_ready, var_ready,
                       rb_ready, w1_ready, w2_ready],
            "scalar": [gx_ready, gc_out, gk_ready, gT_a, gp_ready, gt_a, go_out, xs_ready, sq_ready, v_out, t_out, p_ready, pt_ready, o_out, fsq_ready, gel_ready],
            "vector": [rot_step, gq_ready, gT_v, gtop_ready, gt_v, gon_step, gon_ready, gx_added, qn_ready, cos_ready, s_taken, block_ready, y_ready, norm_step, soft_step,
                       xc_ready, diag_ready, xn_ready, hid_ready, x_ready, var_step, aff_step],
            "gpsimd": [lo_ready, w_hi, w_split, sin_ready, rot_ready, turn_ready, k_kept],
        }

        def done(unit, per=1, part=0):
            return unit * per + part + 1 + CREDIT

        def mean_bank(c):
            return 3 if c else 0

        def var_bank(c):
            return 4 if c else 1

        def spread_bank(c):
            return 4 if c else 2

        def down_bank(c):
            return 5 if c + 1 < CHUNKS else 7

        def kept_by(layer, i, n):
            return (layer * NT + 2 * i + n // 2 + 1) * 16

        def plain(eng):
            eng.sem_inc(passed_sp if eng is nc.sync else passed_pool, 1)

        def rsqrt(v, x, tmp, step, first, op0, c0, op1, c1, between=()):
            u, h, a, y = tmp
            n = [0]
            pieces = iter(between)

            def link(ins):
                ins.then_inc(step, 1)
                n[0] += 1
                piece = next(pieces, None)
                if piece:
                    piece()
                v.wait_ge(step, first + n[0])

            if op1 is None:
                link(v.tensor_scalar(h, x, c0, -0.5, op0, ALU.mult))
                link(v.tensor_scalar(y.bitcast(i32), h.bitcast(i32), -0.5,
                                     1597463007.0 - 2.0 ** 30 - 2.0 ** 22, ALU.mult, ALU.add))
            else:
                link(v.tensor_scalar(u, x, c0, c1, op0, op1))
                v.tensor_scalar(h, u, -0.5, None, ALU.mult)
                link(v.tensor_scalar(y.bitcast(i32), u.bitcast(i32), -0.5, 1597463007.0, ALU.mult, ALU.add))
            for _ in range(3):
                link(v.tensor_tensor(a, y, h, ALU.mult))
                link(v.tensor_tensor(a, a, y, ALU.mult))
                link(v.scalar_tensor_tensor(y, a, 1.5, y, ALU.add, ALU.mult))
        RSQRT = 11

        with nc.Block() as block:
            @block.sync
            def _(sp):
                sp.dma_start(x_tok[:], x_in.rearrange("b (t p) d -> p (b t) d", p=P)).then_inc(w_const, 16)
                sp.dma_start(squares[:], square_in).then_inc(w_const, 16)
                sp.dma_start(rotary[:], rotary_in).then_inc(w_const, 16)
                sp.dma_start(pool[:, layers_end:layers_end + NT * 2 * WIN], mask_in).then_inc(w_const, 16)
                sp.wait_ge(w_const, 64)

            @block.vector
            def _(v):
                for s in counted["vector"]:
                    v.sem_inc(s, CREDIT)
                v.wait_ge(w_const, 64)
                v.tensor_copy(ident_b[:], ident)
                v.memset(causal_b[:, 0:3 * P], 0.0)
                v.tensor_copy(causal_b[:, 3 * P:4 * P], squares[:, 2, :])
                v.tensor_copy(band_b[:].rearrange("p t k -> p (t k)"),
                              pool[:, layers_end:layers_end + NT * 2 * WIN]).then_inc(set_up, 1)
                v.memset(ones[:], 1.0)
                v.memset(mean_w[:], 1.0 / D).then_inc(set_up, 1)

            @block.scalar
            def _(a):
                for s in counted["scalar"]:
                    a.sem_inc(s, CREDIT)

            @block.tensor
            def _(pe):
                for s in counted["tensor"]:
                    pe.sem_inc(s, CREDIT)

            @block.gpsimd
            def _(g):
                for s in counted["gpsimd"]:
                    g.sem_inc(s, CREDIT)
                g.memset(X[:], 0.0)
                g.memset(Y[:], 0.0).then_inc(set_up, 1)

        def load_projections(sp, l):
            sp.dma_start(wqkv, wqkv_in[bass.ds(l, 1)].rearrange("a p n -> p (a n)")).then_inc(w_attn, 16)
            sp.dma_start(scales, scale_in[bass.ds(l, 1)].rearrange("a p n -> p (a n)")).then_inc(w_attn, 16)

        def round_weights(copy, layer):
            copy(wqkv_hi[:], wqkv).then_inc(w_hi, 1)

        def rest_of_weights(g, layer):
            g.wait_ge(w_hi, done(layer))
            plain(g)
            g.tensor_tensor(wqkv_lo[:], wqkv, wqkv_hi[:], ALU.subtract).then_inc(w_split, 1)

        def tables(eng, layer):
            eng.wait_ge(cos_ready, done(layer * UNITS - 1, 2, 1))
            eng.wait_ge(sin_ready, done(layer * UNITS - 1, 2, 1))
            eng.tensor_tensor(turn.rearrange("p t a e -> p t (a e)"),
                              rotary[:].rearrange("p t a e -> p t (a e)"),
                              scales.unsqueeze(1).broadcast_to([P, NT, 4 * DH]),
                              ALU.mult).then_inc(turn_ready, 1)
            eng.wait_ge(turn_ready, done(layer))

        ln_count = [0]

        def layer_norm_tokens(to_skewed):
            r = ln_count[0]
            ln_count[0] += 1
            base = r * (RSQRT + 5)
            ln_x, ln_q = ln_parts[int(to_skewed)]
            L0 = 0 if r == 0 else DEPTH
            with nc.Block() as block:
                @block.gpsimd
                def _(g):
                    if to_skewed:
                        for t in kT + v_last + V + [pT, pT_last]:
                            last = g.memset(t, 0.0)
                        last.then_inc(set_up, 1)
                        rest_of_weights(g, L0)
                    else:
                        for t in g_q + g_k:
                            g.memset(t, 0.0)
                        g.memset(g_v, 0.0).then_inc(g_zero, 1)
                        g.wait_ge(g_zero, 1)
                        g.memset(g_v[:, :, :, MA_D:MA_D + 1], 1.0).then_inc(g_zero, 1)

                @block.sync
                def _(sp):
                    if to_skewed:
                        load_projections(sp, 0)
                    else:
                        for a, b in ((g_down, ma_down_in), (g_up, ma_up_in), (g_qw, ma_q_in), (g_wo, ma_o_in),
                                     (g_tab, ma_rotary_in)):
                            sp.dma_start(a, b).then_inc(w_global, 16)

                @block.vector
                def _(v):
                    if to_skewed:
                        v.memset(Y[64:128, :, 0:1], 0.0)
                    n = [base]

                    def link(ins):
                        ins.then_inc(ln_step, 1)
                        n[0] += 1
                        v.wait_ge(ln_step, n[0])

                    wide = [P, B * NT, D]
                    link(v.tensor_reduce(ln_a[:], x_tok[:], AX.X, ALU.add))
                    link(v.tensor_scalar(ln_a[:], ln_a[:], -1.0 / D, None, ALU.mult))
                    link(v.tensor_tensor(ln_x, x_tok[:], ln_a[:].unsqueeze(2).broadcast_to(wide), ALU.add))
                    link(v.tensor_tensor(ln_q, ln_x, ln_x, ALU.mult))
                    link(v.tensor_reduce(ln_a[:], ln_q, AX.X, ALU.add))
                    rsqrt(v, ln_a[:], [t[:] for t in ln_s], ln_step, n[0], ALU.mult, 1.0 / D, ALU.add, 1e-5)
                    v.tensor_tensor(ln_x, ln_x, ln_s[3][:].unsqueeze(2).broadcast_to(wide),
                                    ALU.mult).then_inc(ln_ready, 1)
                    if to_skewed:
                        v.wait_ge(w_attn, (L0 + 1) * 32)
                        tables(v, L0)

                @block.tensor
                def _(pe):
                    pe.wait_ge(ln_ready, r + 1)
                    for j in range(B * NT):
                        t = pe.transpose(psum[:, P * j:P * j + P], ln_x[:, j, :], ident)
                        if j % 4 == 3:
                            t.then_inc(ln_T, 1)

                @block.scalar
                def _(a):
                    if to_skewed:
                        a.wait_ge(w_attn, (L0 + 1) * 32)
                        round_weights(a.copy, L0)
                    for j in range(4):
                        a.wait_ge(ln_T, 4 * r + j + 1)
                        b, c = j // 2, CHUNK * (j % 2)
                        if to_skewed:
                            a.copy(X[0:64, b, c:c + CHUNK], bank(j)[0:64, :])
                            a.copy(X[64:128, b, c + 1:c + 1 + CHUNK], bank(j)[64:128, :])
                        else:
                            a.copy(Y[:, b, c:c + CHUNK], bank(j))

        def attention(eng, step):
            for k in range(3):
                step(0, k, lambda d, k=k: k - d >= 0)
            with eng.Fori(0, 3) as i:
                for k in range(3, 7):
                    step(i, k, lambda d: True)
            step(3, 3, lambda d: d >= 0)

        def layers(half):
            with nc.Block() as block:
                L0 = DEPTH * half

                @block.sync
                def _(sp):
                    def layer(l):
                        U0, C0 = (l + L0) * UNITS, (l + L0) * CHUNKS
                        sp.wait_ge(wo_ready, done(U0 - 1))
                        plain(sp)
                        sp.dma_start(wo, wo_in[bass.ds(l, 1)].rearrange("a p c n -> p (a c) n")).then_inc(w_out, 16)
                        sp.wait_ge(x_ready, done(C0 - 1))
                        plain(sp)
                        sp.dma_start(w1, w1_in[bass.ds(l, 1)].rearrange("a p n -> p (a n)")).then_inc(w_ffn, 16)
                        sp.dma_start(w2, w2_in[bass.ds(l, 1)].rearrange("a p c n -> p (a c) n")).then_inc(w_ffn, 16)
                        sp.dma_start(vec, vec_in[bass.ds(l, 1)].rearrange("a p n -> p (a n)")).then_inc(w_ffn, 16)

                        def step(i, k, has):
                            U = U0 + 4 * i + k
                            if has(0):
                                sp.wait_ge(o_ready, done(U - 2))
                                sp.wait_ge(v_out, done(U - 2))
                                plain(sp)
                                sp.dma_start(v_last[k % 2][96:128, :],
                                             V[(k - 2) % 4][96:128, :]).then_inc(kept[k % 2], 16)

                        attention(sp, step)

                    with sp.Fori(0, DEPTH - 1) as l:
                        layer(l)
                        last = (l + L0) * UNITS + UNITS - 1
                        sp.wait_ge(turn_ready, done(l + L0))
                        plain(sp)
                        sp.wait_ge(sin_ready, done(last, 2, 1))
                        sp.wait_ge(cos_ready, done(last, 2, 1))
                        plain(sp)
                        load_projections(sp, l + 1)
                    layer(DEPTH - 1)

                @block.tensor
                def _(pe):
                    with pe.Fori(0, DEPTH) as l:
                        U0, C0 = (l + L0) * UNITS, (l + L0) * CHUNKS

                        def output(V0, k):
                            pe.wait_ge(o_out, done(V0 + k, 2, 1))
                            for c in range(PAIRS):
                                last = pe.matmul(bank(7)[:, 0:P], wo[:, c, :], oT[:, c, :],
                                                 start=(c == 0), stop=(c == PAIRS - 1))
                            last.then_inc(wo_ready, 1)

                        def turned_scores(V0, i, k, v_behind, between=None, middle=None):
                            U = V0 + k
                            pe.wait_ge(rot_ready, done(U, 2, 0))
                            if isinstance(i, int) and i == 0 and k == 0:
                                pe.wait_ge(x_ready, done(C0 - 1))
                            for p in range(4):
                                if p == 1:
                                    pe.wait_ge(o_out, done(U - 2, 2, 1))
                                if p == 2:
                                    if middle:
                                        middle()
                                    pe.wait_ge(rot_ready, done(U, 2, 1))
                                if p >= 2:
                                    pe.wait_ge(t_out, done(U, 4, p - 2))
                                for j in range(4):
                                    c = 4 * (p % 2) + j
                                    last = pe.transpose(bank(7 - p % 2)[:, P * j:P * j + P],
                                                        rot[:, p // 2, 2 * c:2 * c + 2, :], ident)
                                last.then_inc(t_ready, 1)
                            if between:
                                between()
                            pe.wait_ge(v_out, done(U + 1 if v_behind else U))
                            if not v_behind:
                                pe.wait_ge(s_taken, done(U - 1))
                            band = band_b[:, bass.ds(2 * i + k // 2, 1), :].broadcast_to([P, HEADS // 2, 2 * WIN])
                            for j in range(2):
                                pe.matmul(bank(4 + j), ident_b[:], band, start=True, stop=False)
                            pe.wait_ge(k_kept, done(U))
                            for c in range(PAIRS):
                                if c % 4 == 0:
                                    pe.wait_ge(t_out, done(U, 4, 2 + c // 4))
                                for w in range(NW):
                                    o = bank(4 + c // 4)[WIN * w:WIN * w + WIN, P * (c % 4):P * (c % 4) + P]
                                    last = pe.matmul(o, qT[:, c, WIN * w:WIN * w + WIN],
                                                     kT[k % 2][:, c, :, WIN * w:WIN * w + 2 * WIN],
                                                     start=False, stop=(c % 4 == 3))
                            last.then_inc(s_ready, 1)

                        def values(V0, i, k):
                            U = V0 + k
                            pe.wait_ge(pt_ready, done(U))
                            pe.wait_ge(y_ready, done(U - 1))
                            pe.wait_ge(kept[k % 2], kept_by(l + L0, i, k))
                            for h in range(HEADS):
                                r = 64 * (h % 2)
                                o = bank(6 + h // 8)[r:r + 64, P * (h // 2 % 4):P * (h // 2 % 4) + P]
                                pe.matmul(o, V[k % 4][:, DH * h:DH * h + DH], pT[:, h, :], start=True, stop=False)
                                last = pe.matmul(o[:, 0:WIN], v_last[k % 2][:, DH * h:DH * h + DH],
                                                 pT_last[:, h, :], start=False, stop=True)
                            last.then_inc(o_ready, 1)

                        def step(i, k, has):
                            U = U0 + 4 * i + k
                            def three_passes(o, c):
                                pe.matmul(o, xs_lo[:, k % 2, :], wqkv_hi[:, c], start=True, stop=False)
                                pe.matmul(o, xs_hi[:, k % 2, :], wqkv_lo[:, c], start=False, stop=False)
                                return pe.matmul(o, xs_hi[:, k % 2, :], wqkv_hi[:, c], start=False, stop=True)

                            def v_products(parts=range(2)):
                                pe.wait_ge(lo_ready, done(U))
                                pe.wait_ge(s_taken, done(U - 2))
                                if not has(2):
                                    pe.wait_ge(v_out, done(U - 1))
                                for j in parts:
                                    last = three_passes(bank(4 + j), slice(2 * INNER + 512 * j,
                                                                           2 * INNER + 512 * j + 512))
                                if 1 in parts:
                                    last.then_inc(v_ready, 1)

                            early = has(1) and not has(2)
                            if early:
                                v_products()
                            if has(0):
                                if k == 0:
                                    pe.wait_ge(w_split, done(l + L0))
                                pe.wait_ge(lo_ready, done(U))
                                for j in range(4):
                                    if j % 2 == 0:
                                        pe.wait_ge(qn_ready, done(U - 1, 2, j // 2))
                                    last = three_passes(bank(j), slice(512 * j, 512 * j + 512))
                                    if j % 2:
                                        last.then_inc(qk_ready, 1)
                            if has(3):
                                values(U0 + 4 * i, i, k - 3)
                            if has(0) and not early:
                                v_products(range(1) if has(3) else range(2))
                            if has(3):
                                pe.wait_ge(o_out, done(U - 3, 2, 0))

                            def behind():
                                if k == 3:
                                    pe.wait_ge(w_out, (l + L0 + 1) * 16)
                                pe.wait_ge(t_out, done(U - 1, 4, 2))
                                output(U0 + 4 * i, k - 3)

                            if has(1):
                                turned_scores(U0 + 4 * i, i, k - 1, has(0), between=behind if has(3) else None,
                                              middle=(lambda: v_products((1,))) if has(3) else None)

                        attention(pe, step)

                        def mean(c):
                            pe.wait_ge(y_ready, done(U0 + 2 * (4 * (c // 2) + 3) + c % 2))
                            if c == 0:
                                pe.wait_ge(qn_ready, done(U0 + UNITS - 1, 2, 1))
                            else:
                                pe.wait_ge(hid_ready, done(C0 + c - 2, NF, 1))
                            pe.matmul(bank(mean_bank(c)), mean_w[:], Y[:, c % 2, CHUNK * (c // 2):CHUNK * (c // 2) + CHUNK],
                                      start=True, stop=True).then_inc(mu_ready, 1)

                        def variance(c):
                            pe.wait_ge(fsq_ready, done(C0 + c))
                            if c == 1:
                                pe.wait_ge(s_taken, done(U0 + UNITS - 1))
                            if c > 1:
                                pe.wait_ge(xn_ready, done(C0 + c - 1))
                            for j in range(CHUNK // P):
                                last = pe.matmul(bank(var_bank(c))[:, j:j + 1], fsq[:, P * j:P * j + P], mean_w[:, 0:1],
                                                 start=True, stop=True)
                            last.then_inc(var_ready, 1)

                        def spread(c):
                            pe.wait_ge(diag_ready, done(C0 + c))
                            pe.matmul(bank(spread_bank(c)), ones[:], diag.rearrange("p a b -> p (a b)"),
                                      start=True, stop=True).then_inc(rb_ready, 1)

                        def up(c, j):
                            C = C0 + c
                            if j == 0:
                                pe.wait_ge(xn_ready, done(C))
                            pe.wait_ge(hid_ready, done(C, NF, j - 2))
                            if j == 1 and c + 1 < CHUNKS:
                                pe.wait_ge(xc_ready, done(C + 1))
                            m = FP[j]
                            pe.matmul(bank(2 * (j % 2))[0:m, :], w1[:, P * j:P * j + m], xn, start=True, stop=True)
                            pe.matmul(bank(2 * (j % 2) + 1)[0:m, :], w1[:, F + P * j:F + P * j + m], xn,
                                      start=True, stop=True).then_inc(w1_ready, 1)

                        def down(c, pieces):
                            C = C0 + c
                            for j in pieces:
                                pe.wait_ge(hid_ready, done(C, NF, j))
                                last = pe.matmul(bank(down_bank(c)), w2[0:FP[j], j, :], hid[j][0:FP[j], :],
                                                 start=(j == 0), stop=(j == NF - 1))
                            if j == NF - 1:
                                last.then_inc(w2_ready, 1)

                        W0 = U0 + 12
                        mean(0)
                        values(W0, 3, 1)

                        def behind():
                            variance(0)
                            pe.wait_ge(t_out, done(W0 + 3, 4, 2))
                            output(W0, 1)

                        pe.wait_ge(o_out, done(W0 + 1, 2, 0))
                        turned_scores(W0, 3, 3, False, between=behind)
                        spread(0)
                        values(W0, 3, 2)
                        pe.wait_ge(w_ffn, (l + L0 + 1) * 48)
                        for c in range(CHUNKS):
                            more = c + 1 < CHUNKS
                            if more:
                                mean(c + 1)
                            up(c, 0)
                            if c < 2:
                                output(W0, 2 + c)
                            if more:
                                variance(c + 1)
                            up(c, 1)
                            up(c, 2)
                            down(c, (0,))
                            if more:
                                spread(c + 1)
                            down(c, range(1, NF - 1))
                            if c == 0:
                                values(W0, 3, 3)
                            down(c, (NF - 1,))

                @block.scalar
                def _(a):
                    with a.Fori(0, DEPTH) as l:
                        U0, C0 = (l + L0) * UNITS, (l + L0) * CHUNKS

                        def take(i, n):
                            U = U0 + 4 * i + n
                            a.wait_ge(v_ready, done(U - 2))
                            a.wait_ge(qk_ready, done(U - 2, 2, 1))
                            c = n if isinstance(i, int) and 4 * i + n < 2 else CHUNKS - 1
                            a.wait_ge(x_ready, done(C0 - CHUNKS + c))
                            t = 2 * i + n // 2
                            a.copy(xs[:, n % 2, :], X[:, n % 2, bass.ds(t * P, P)])
                            a.copy(xs_hi[:, n % 2, :], X[:, n % 2, bass.ds(t * P, P)]).then_inc(xs_ready, 1)

                        def turned(U, k, parts):
                            a.wait_ge(s_ready, done(U - 1))
                            for p in parts:
                                a.wait_ge(t_ready, done(U, 4, p))
                                if p < 2:
                                    a.copy(qT[:, 4 * p:4 * p + 4, :].rearrange("p c t -> p (c t)"),
                                           bank(7 - p)).then_inc(t_out, 1)
                                    continue
                                if p == 2:
                                    a.wait_ge(k_kept, done(U))
                                c = 4 * (p - 2)
                                for r in range(2):
                                    last = a.copy(kT[k % 2][64 * r:64 * r + 64, c:c + 4, r, WIN:WIN + P],
                                                  bank(7 - p % 2)[64 * r:64 * r + 64, :]
                                                  .rearrange("p (c t) -> p c t", c=4))
                                last.then_inc(t_out, 1)

                        def diagonal(U):
                            a.wait_ge(block_ready, done(U))
                            a.wait_ge(o_ready, done(U - 1))
                            a.copy(pT_last[96:128, :, :], turned_P[0:WIN, :, 0:WIN])
                            for w in range(NW):
                                rows = slice(WIN * w, WIN * w + WIN)
                                if w:
                                    a.copy(pT[WIN * (w - 1):WIN * w, :, rows], turned_P[rows, :, 0:WIN])
                                last = a.copy(pT[rows, :, rows], turned_P[rows, :, WIN:2 * WIN])
                            last.then_inc(pt_ready, 1)

                        def exponents(U):
                            a.wait_ge(s_taken, done(U))
                            a.activation(S, S, ACT.Exp).then_inc(p_ready, 1)

                        def products(U):
                            a.wait_ge(o_ready, done(U))
                            a.wait_ge(wo_ready, done(U - 1))
                            for j in (1, 0):
                                a.copy(oT[:, 4 * j:4 * j + 4, :].rearrange("p c t -> p (c t)"),
                                       bank(6 + j)).then_inc(o_out, 1)

                        take(0, 0)

                        def step(i, k, has):
                            U = U0 + 4 * i + k
                            if has(0):
                                for q in range(2):
                                    a.wait_ge(qk_ready, done(U, 2, q))
                                    if q == 0:
                                        a.wait_ge(qn_ready, done(U - 1, 2, 0))
                                    a.activation(sq[:, INNER * q:INNER * (q + 1)], bank(2 * q, 2),
                                                 ACT.Square).then_inc(sq_ready, 1)
                            if has(2):
                                exponents(U0 + 4 * i + k - 2)
                            if has(-1):
                                take(i, k + 1)
                            if has(3):
                                products(U0 + 4 * i + k - 3)
                            if has(1):
                                turned(U0 + 4 * i + k - 1, k - 1, (0, 1, 2) if has(3) else ())
                            if has(0):
                                a.wait_ge(v_ready, done(U))
                                a.wait_ge(o_ready, done(U - 4))
                                if k >= 2:
                                    a.wait_ge(kept[k % 2], kept_by(l + L0, i, k - 2))
                                a.copy(V[k % 4], bank(4, 2)).then_inc(v_out, 1)
                            if has(1):
                                turned(U0 + 4 * i + k - 1, k - 1, (3,) if has(3) else range(4))
                            if has(2):
                                diagonal(U0 + 4 * i + k - 2)
                        attention(a, step)

                        def squares_of(c):
                            a.wait_ge(xc_ready, done(C0 + c))
                            a.activation(fsq, xc, ACT.Square).then_inc(fsq_ready, 1)

                        last = U0 + UNITS - 1
                        exponents(last - 1)
                        products(last - 2)
                        squares_of(0)
                        turned(last, UNITS - 1, range(4))
                        diagonal(last - 1)
                        exponents(last)
                        products(last - 1)
                        a.wait_ge(w_ffn, (l + L0 + 1) * 48)
                        for c in range(CHUNKS):
                            if c + 1 < CHUNKS:
                                squares_of(c + 1)
                            for j in range(NF):
                                C = C0 + c
                                a.wait_ge(w1_ready, done(C, NF, j))
                                a.wait_ge(hid_ready, done(C, NF, j - 2))
                                m = FP[j]
                                a.activation(gel[j % 2][0:m, :], bank(2 * (j % 2) + 1)[0:m, :], ACT.Gelu,
                                             bias=vec[0:m, NF + j:NF + j + 1]).then_inc(gel_ready, 1)
                                if c == 0 and j == 1:
                                    diagonal(last)
                            if c == 0:
                                products(last)

                @block.gpsimd
                def _(g):
                    def layer(l):
                        U0 = (l + L0) * UNITS

                        def rest(U, k):
                            g.wait_ge(xs_ready, done(U))
                            plain(g)
                            g.tensor_tensor(xs_lo[:, k % 2, :], xs[:, k % 2, :], xs_hi[:, k % 2, :],
                                            ALU.subtract).then_inc(lo_ready, 1)

                        def keep(U, k):
                            g.wait_ge(s_ready, done(U - 2))
                            b = kT[k % 2]
                            plain(g)
                            g.tensor_copy(b[:, :, :, 0:WIN], b[:, :, :, P:P + WIN]).then_inc(k_kept, 1)

                        def step(i, k, has):
                            U = U0 + 4 * i + k
                            if has(1):
                                keep(U - 1, k - 1)
                            if has(-1):
                                rest(U + 1, k + 1)
                            if has(0):
                                t = 2 * i + k // 2
                                hd = DH // 2
                                for q in range(2):
                                    g.wait_ge(qn_ready, done(U, 2, q))
                                    g.wait_ge(t_ready, done(U - 1, 4, 2 * q + 1))
                                    plain(g)
                                    for r in range(2):
                                        tab = turn[:, bass.ds(t, 1), 2 + q, hd * r:hd * r + hd].broadcast_to(
                                            [P, HEADS, hd])
                                        last = g.tensor_tensor(rot[:, q, :, hd * r:hd * r + hd],
                                                               qn[:, q, :, hd * (1 - r):hd * (2 - r)], tab, ALU.mult)
                                    last.then_inc(sin_ready, 1)
                                    g.wait_ge(sin_ready, done(U, 2, q))
                                    g.wait_ge(cos_ready, done(U, 2, q))
                                    g.tensor_tensor(rot[:, q], rot[:, q], by_cos[:, q], ALU.add).then_inc(rot_ready, 1)

                        rest(U0, 0)
                        attention(g, step)
                        keep(U0 + UNITS - 1, UNITS - 1)

                    with g.Fori(0, DEPTH - 1) as l:
                        layer(l)
                        g.wait_ge(v_ready, done((l + L0) * UNITS + UNITS - 1))
                        g.wait_ge(w_attn, (l + L0 + 2) * 32)
                        plain(g)
                        round_weights(g.tensor_copy, l + L0 + 1)
                        rest_of_weights(g, l + L0 + 1)
                        tables(g, l + L0 + 1)
                    layer(DEPTH - 1)

                @block.vector
                def _(v):
                    with v.Fori(0, DEPTH) as l:
                        U0, C0 = (l + L0) * UNITS, (l + L0) * CHUNKS

                        def probabilities(U):
                            def sums(part):
                                hs = slice(8 * part, 8 * part + 8)
                                if part == 0:
                                    v.wait_ge(p_ready, done(U))
                                v.tensor_reduce(total[:, hs], S[:, hs, :], AX.X, ALU.add).then_inc(soft_step, 1)

                            def over_sums():
                                v.wait_ge(soft_step, done(U, 5, 2))
                                v.reciprocal(over, total).then_inc(soft_step, 1)

                            def normal_part(part):
                                hs = slice(4 * part, 4 * part + 4)
                                if part == 0:
                                    v.wait_ge(soft_step, done(U, 5, 3))
                                ins = v.tensor_tensor(S[:, hs, :], S[:, hs, :], over[:, hs].unsqueeze(2)
                                                      .broadcast_to([P, 4, 2 * WIN]), ALU.mult)
                                if part == 3:
                                    ins.then_inc(soft_step, 1)

                            def turn_part(part):
                                hs = slice(4 * part, 4 * part + 4)
                                if part == 0:
                                    v.wait_ge(soft_step, done(U, 5, 4))
                                    v.wait_ge(pt_ready, done(U - 1))
                                ins = v.transpose(turned_P[:, hs, :], S[:, hs, :])
                                if part == 3:
                                    ins.then_inc(block_ready, 1)

                            return ([lambda: sums(0), lambda: sums(1), over_sums]
                                    + [lambda part=part: normal_part(part) for part in range(4)]
                                    + [lambda part=part: turn_part(part) for part in range(4)])

                        def residual(U, i, k):
                            t, s = 2 * i + k // 2, k % 2
                            v.wait_ge(wo_ready, done(U))
                            v.tensor_tensor(Y[0:64, s, bass.ds(t * P, P)], bank(7)[0:64, 0:P],
                                            X[0:64, s, bass.ds(t * P, P)], ALU.add)
                            v.tensor_tensor(Y[64:128, s, bass.ds(t * P + 1, P)], bank(7)[64:128, 0:P],
                                            X[64:128, s, bass.ds(t * P + 1, P)], ALU.add).then_inc(y_ready, 1)

                        def less_top(U):
                            sc = bank(4, 2).rearrange("p (h e) -> p h e", e=2 * WIN)
                            v.wait_ge(s_ready, done(U))
                            v.tensor_reduce(top, sc, AX.X, ALU.max).then_inc(soft_step, 1)
                            v.wait_ge(soft_step, done(U, 5, 0))
                            v.wait_ge(block_ready, done(U - 1))
                            v.tensor_tensor(S, sc, top.unsqueeze(2).broadcast_to([P, HEADS, 2 * WIN]),
                                            ALU.subtract).then_inc(s_taken, 1)

                        def step(i, k, has):
                            U = U0 + 4 * i + k
                            if has(0):
                                t = 2 * i + k // 2
                                for q in range(2):
                                    v.wait_ge(sq_ready, done(U, 2, q))
                                    last = v.tensor_reduce(ss[:, HEADS * q:HEADS * (q + 1)],
                                                           sq[:, INNER * q:INNER * (q + 1)].rearrange(
                                                               "p (h e) -> p h e", e=DH), AX.X, ALU.add)
                                last.then_inc(norm_step, 1)
                                v.wait_ge(norm_step, done(U, RSQRT + 1, 0))
                                rsqrt(v, ss, nwt, norm_step, done(U, RSQRT + 1, 0), ALU.max, 1e-24, None, None,
                                      between=probabilities(U - 2) if has(2) else ())
                                v.wait_ge(sin_ready, done(U - 1, 2, 1))
                                v.wait_ge(cos_ready, done(U - 1, 2, 1))
                                for q in range(2):
                                    v.tensor_tensor(qn[:, q], bank(2 * q, 2).rearrange("p (h e) -> p h e", e=DH),
                                                    nwt[3][:, HEADS * q:HEADS * (q + 1)].unsqueeze(2)
                                                    .broadcast_to([P, HEADS, DH]), ALU.mult).then_inc(qn_ready, 1)
                                if has(3):
                                    residual(U - 3, i, k - 3)
                                if k == 0:
                                    v.wait_ge(turn_ready, done(l + L0))
                                v.wait_ge(qn_ready, done(U, 2, 1))
                                v.wait_ge(rot_ready, done(U - 1, 2, 1))
                                for q in range(2):
                                    tab = turn[:, bass.ds(t, 1), q, :].broadcast_to([P, HEADS, DH])
                                    v.tensor_tensor(by_cos[:, q], qn[:, q], tab, ALU.mult).then_inc(cos_ready, 1)
                            if has(1):
                                less_top(U - 1)

                        attention(v, step)

                        def centre(c):
                            v.wait_ge(mu_ready, done(C0 + c))
                            v.tensor_tensor(xc, Y[:, c % 2, CHUNK * (c // 2):CHUNK * (c // 2) + CHUNK], bank(mean_bank(c)),
                                            ALU.subtract).then_inc(xc_ready, 1)

                        def deviation(c, between=()):
                            v.wait_ge(var_ready, done(C0 + c))
                            rsqrt(v, bank(var_bank(c))[:, 0:CHUNK // P], var, var_step, done(C0 + c, RSQRT, -1),
                                  ALU.mult, 1.0, ALU.add, 1e-5, between=between)
                            for j in range(CHUNK // P):
                                last = v.tensor_scalar(diag[:, j, :], ident, var[3][:, j:j + 1], None, ALU.mult)
                            last.then_inc(diag_ready, 1)

                        def normal(c):
                            v.wait_ge(rb_ready, done(C0 + c))
                            v.tensor_tensor(xn, xc, bank(spread_bank(c)), ALU.mult).then_inc(aff_step, 1)
                            v.wait_ge(aff_step, done(C0 + c))
                            v.tensor_scalar(xn, xn, vec[:, 2 * NF:2 * NF + 1], vec[:, 2 * NF + 1:2 * NF + 2],
                                            ALU.mult, ALU.add).then_inc(xn_ready, 1)

                        def hidden(c, j):
                            m = FP[j]
                            v.wait_ge(gel_ready, done(C0 + c, NF, j))
                            v.wait_ge(w2_ready, done(C0 + c - 1))
                            v.scalar_tensor_tensor(hid[j][0:m, :], bank(2 * (j % 2))[0:m, :], vec[0:m, j:j + 1],
                                                   gel[j % 2][0:m, :], ALU.add, ALU.mult).then_inc(hid_ready, 1)

                        def result(c):
                            b, at0 = c % 2, CHUNK * (c // 2)
                            v.wait_ge(w2_ready, done(C0 + c))
                            for r in range(2):
                                rows = slice(64 * r, 64 * r + 64)
                                last = v.scalar_tensor_tensor(
                                    X[rows, b, at0 + r:at0 + r + CHUNK], bank(down_bank(c))[rows, :],
                                    vec[rows, 2 * NF + 2:2 * NF + 3], Y[rows, b, at0 + r:at0 + r + CHUNK],
                                    ALU.add, ALU.add)
                            last.then_inc(x_ready, 1)

                        W0 = U0 + 12
                        centre(0)
                        for piece in probabilities(W0 + 2):
                            piece()
                        deviation(0)
                        residual(W0 + 1, 3, 1)
                        v.wait_ge(w_ffn, (l + L0 + 1) * 48)
                        less_top(W0 + 3)
                        normal(0)
                        for piece in probabilities(W0 + 3):
                            piece()
                        for c in range(CHUNKS):
                            more = c + 1 < CHUNKS
                            if more:
                                centre(c + 1)
                            hidden(c, 0)
                            if c < 2:
                                residual(W0 + 2 + c, 3, 2 + c)
                            if more:
                                deviation(c + 1)
                            for j in range(1, NF):
                                hidden(c, j)
                            if more:
                                normal(c + 1)
                            result(c)

        def add_half(half):
            with nc.Block() as block:
                @block.scalar
                def _(a):
                    for b in range(B):
                        a.copy(Y[0:64, b, 0:T], X[0:64, b, 0:T])
                        a.copy(Y[64:128, b, 0:T], X[64:128, b, 1:T + 1]).then_inc(flat_ready, 1)

                @block.tensor
                def _(pe):
                    for j in range(B * NT):
                        if j % NT == 0:
                            pe.wait_ge(flat_ready, B * half + j // NT + 1)
                        t = pe.transpose(psum[:, P * j:P * j + P], Y[:, j // NT, P * (j % NT):P * (j % NT) + P], ident)
                        if j % 4 == 3:
                            t.then_inc(flat_T, 1)

                @block.vector
                def _(v):
                    for j in range(4):
                        v.wait_ge(flat_T, 4 * half + j + 1)
                        x = x_tok[:, 4 * j:4 * j + 4, :].rearrange("p a d -> p (a d)")
                        v.scalar_tensor_tensor(x, bank(j), 0.5, x, ALU.mult, ALU.add)

        def global_attention():
            HS = NT * MA_H
            pieces = [(g, p) for g in range(HS) for p in range(g // MA_H // 4 + 1)]
            number = {gp: n for n, gp in enumerate(pieces)}
            by_a = [n % 2 == 0 for n in range(len(pieces))]

            def moved(b, n):
                own = [m for m in range(len(pieces)) if by_a[m] == by_a[n]]
                return (gt_a if by_a[n] else gt_v), done(b, len(own), own.index(n))

            def piece_out(eng, copy, b, g, p, n):
                t, h = divmod(g, MA_H)
                eng.wait_ge(gt_ready, done(b, len(pieces), n))
                if g >= 2:
                    eng.wait_ge(gpv_ready, done(b, HS, g - 2))
                m = P * min(4, t + 1 - 4 * p)
                return copy(g_pT[h % 2][:, 512 * p:512 * p + m], bank(4 + p)[:, 0:m])

            with nc.Block() as block:
                @block.tensor
                def _(pe):
                    pe.wait_ge(w_global, 80)
                    with pe.Fori(0, B) as b:
                        pe.wait_ge(gx_ready, done(b))
                        for j in range(2):
                            last = pe.matmul(bank(j), g_down, g_x[:, 512 * j:512 * j + 512], start=True, stop=True)
                        last.then_inc(gc_ready, 1)
                        pe.wait_ge(gc_out, done(b))

                        def project(t):
                            o, o2 = bank(2 * (t % 2)), bank(2 * (t % 2) + 1)
                            if t >= 2:
                                pe.wait_ge(gq_ready, done(b, NT, t - 2))
                                pe.wait_ge(gk_ready, done(b, NT, t - 2))
                            c = slice(P * t, P * t + P)
                            pe.matmul(o[:, 0:2 * D], g_c[:, c], g_up[:, 0:2 * D], start=True, stop=True)
                            pe.matmul(o2[:, 0:MA_R], g_c[:, c], g_up[:, 2 * D:2 * D + MA_R], start=True, stop=True)
                            pe.matmul(o2[:, MA_R:D + 2 * MA_R], g_x[:, c], g_qw,
                                      start=True, stop=True).then_inc(proj_ready, 1)

                        def turn_over(t):
                            pe.wait_ge(gq_ready, done(b, NT, t))
                            pe.wait_ge(gk_ready, done(b, NT, t))
                            for p in range(4):
                                if t:
                                    pe.wait_ge((gT_a, gT_v)[p % 2], done(b, 2 * NT, 2 * (t - 1) + p // 2))
                                for j in range(4):
                                    c = 4 * (p % 2) + j
                                    last = pe.transpose(bank(4 + p)[:, P * j:P * j + P],
                                                        (g_q, g_k)[p // 2][t % 2][:, 2 * c:2 * c + 2, :], ident)
                                last.then_inc(gT_ready, 1)

                        project(0)
                        for t in range(NT):
                            if t + 1 < NT:
                                project(t + 1)
                            turn_over(t)
                        pe.wait_ge(gT_a, done(b, 2 * NT, 2 * NT - 1))
                        pe.wait_ge(gT_v, done(b, 2 * NT, 2 * NT - 1))

                        def scores(g):
                            t, h = divmod(g, MA_H)
                            if g >= 2:
                                pe.wait_ge(gp_ready, done(b, HS, g - 2))
                            r, c = 64 * (h % 2), h // 2
                            q = g_qT[r:r + 64, c, P * t:P * t + P]
                            for j in range(t // 4 + 1):
                                n = min(P * (t + 1) - 512 * j, 512)
                                o = bank(2 * (h % 2) + j)
                                diagonal = 512 * j <= P * t < 512 * j + n
                                if diagonal:
                                    pe.matmul(o[:, 0:n], ident_b[:], causal_b[:, 512 - n:512],
                                              start=True, stop=False)
                                last = pe.matmul(o[:, 0:n], q, g_kT[r:r + 64, c, 512 * j:512 * j + n],
                                                 start=not diagonal, stop=True)
                            last.then_inc(gs_ready, 1)

                        def probabilities(g):
                            t, h = divmod(g, MA_H)
                            pe.wait_ge(gp_ready, done(b, HS, g))
                            for p in range(t // 4 + 1):
                                if (g - 1, p) in number:
                                    pe.wait_ge(*moved(b, number[g - 1, p]))
                                for j in range(min(4, t + 1 - 4 * p)):
                                    k = 4 * p + j
                                    last = pe.transpose(bank(4 + p)[:, P * j:P * j + P],
                                                        g_p[h % 2][:, P * k:P * k + P], ident)
                                last.then_inc(gt_ready, 1)

                        def values(g):
                            t, h = divmod(g, MA_H)
                            for p in range(t // 4 + 1):
                                pe.wait_ge(*moved(b, number[g, p]))
                            if h == 0 and t:
                                pe.wait_ge(go_out, done(b, NT, t - 1))
                            for k in range(t + 1):
                                last = pe.matmul(bank(6)[WIN * (h % 4):WIN * (h % 4) + WIN, P * (h // 4):P * (h // 4) + P],
                                                 g_v[:, k, h, :], g_pT[h % 2][:, P * k:P * k + P],
                                                 start=(k == 0), stop=(k == t))
                            last.then_inc(gpv_ready, 1)

                        def sums(t):
                            pe.wait_ge(go_out, done(b, NT, t))
                            if t:
                                pe.wait_ge(gx_added, done(b, NT, t - 1))
                            pe.matmul(bank(7), squares[:, 1, :], g_o, start=True, stop=True).then_inc(gsum_ready, 1)

                        def project_out(t):
                            pe.wait_ge(gon_ready, done(b, NT, t))
                            for j in range(4):
                                last = pe.matmul(bank(7)[:, 0:P], g_on[:, P * j:P * j + P], g_wo[:, j, :],
                                                 start=(j == 0), stop=(j == 3))
                            last.then_inc(gwo_ready, 1)

                        scores(0)
                        for g in range(HS + 1):
                            t, h = divmod(g, MA_H)
                            if g + 1 < HS:
                                scores(g + 1)
                            if g < HS:
                                probabilities(g)
                            if g:
                                values(g - 1)
                            if t and g < HS and h == 2:
                                sums(t - 1)
                            if t and g < HS and h == 5:
                                project_out(t - 1)
                        sums(NT - 1)
                        project_out(NT - 1)

                @block.scalar
                def _(a):
                    a.wait_ge(g_zero, 2)
                    with a.Fori(0, B) as b:
                        a.copy(g_x, Y[:, bass.ds(b, 1), 0:T].rearrange("p a t -> p (a t)")).then_inc(gx_ready, 1)
                        a.wait_ge(gc_ready, done(b))
                        a.copy(g_c, bank(0, 2)).then_inc(gc_out, 1)

                        def out_of(t):
                            for p in (0, 2):
                                a.wait_ge(gT_ready, done(b, 4 * NT, 4 * t + p))
                                a.copy((g_qT, g_kT)[p // 2][:, 0:4, P * t:P * t + P],
                                       bank(4 + p).rearrange("p (c t) -> p c t", c=4)).then_inc(gT_a, 1)

                        for t in range(NT):
                            a.wait_ge(proj_ready, done(b, NT, t))
                            if t >= 2:
                                a.wait_ge(gT_ready, done(b, 4 * NT, 4 * (t - 2) + 3))
                            o = bank(2 * (t % 2))
                            heads = "p (h e) -> p h e"
                            a.copy(g_v[:, t, :, 0:MA_D], o[:, D:2 * D].rearrange(heads, e=MA_D))
                            a.copy(g_k[t % 2][:, :, 0:MA_D], o[:, 0:D].rearrange(heads, e=MA_D)).then_inc(gk_ready, 1)
                            if t:
                                out_of(t - 1)
                        out_of(NT - 1)
                        for g in range(HS + 1):
                            t, h = divmod(g, MA_H)
                            if g < HS:
                                a.wait_ge(gtop_ready, done(b, HS, g))
                                if g >= 2:
                                    a.wait_ge(gt_ready, done(b, len(pieces), number[g - 2, (g - 2) // MA_H // 4]))
                                a.activation(g_p[h % 2][:, 0:P * (t + 1)], bank(2 * (h % 2), 2)[:, 0:P * (t + 1)],
                                             ACT.Exp, bias=g_top[h % 2]).then_inc(gp_ready, 1)
                                for p in range(t // 4 + 1):
                                    n = number[g, p]
                                    if by_a[n]:
                                        piece_out(a, a.copy, b, g, p, n).then_inc(gt_a, 1)
                            if t and h == 0:
                                a.wait_ge(gpv_ready, done(b, HS, g - 1))
                                a.wait_ge(gwo_ready, done(b, NT, t - 2))
                                a.copy(g_o, bank(6)).then_inc(go_out, 1)

                @block.vector
                def _(v):
                    v.wait_ge(w_global, 80)
                    v.wait_ge(g_zero, 2)
                    with v.Fori(0, B) as b:
                        def out_of(t):
                            for p in (1, 3):
                                v.wait_ge(gT_ready, done(b, 4 * NT, 4 * t + p))
                                v.tensor_copy((g_qT, g_kT)[p // 2][:, 4:8, P * t:P * t + P],
                                              bank(4 + p).rearrange("p (c t) -> p c t", c=4)).then_inc(gT_v, 1)

                        for t in range(NT):
                            o = bank(2 * (t % 2) + 1)
                            hr = MA_R // 2
                            v.wait_ge(proj_ready, done(b, NT, t))
                            pair = o[:, 0:2 * MA_R].rearrange("p (a e) -> p a e", e=hr)
                            for r in range(2):
                                last = v.tensor_tensor(
                                    g_rot[t % 2][:, 2 * r:2 * r + 2, :].rearrange("p a (x e) -> p (a x) e", e=hr), pair,
                                    g_tab[:, t, r:r + 1, :].broadcast_to([P, 4, hr]), ALU.mult)
                            last.then_inc(rot_step, 1)
                            v.wait_ge(rot_step, done(b, 2 * NT, 2 * t))
                            c, s, new = g_rot[t % 2][:, 0:2, :], g_rot[t % 2][:, 2:4, :], g_new[t % 2]
                            v.tensor_tensor(new[:, :, 0:hr], c[:, :, 0:hr], s[:, :, hr:MA_R], ALU.subtract)
                            v.tensor_tensor(new[:, :, hr:MA_R], c[:, :, hr:MA_R], s[:, :, 0:hr],
                                            ALU.add).then_inc(rot_step, 1)
                            if t >= 2:
                                v.wait_ge(gT_ready, done(b, 4 * NT, 4 * (t - 2) + 3))
                            v.tensor_scalar(g_q[t % 2][:, :, 0:MA_D],
                                            o[:, 2 * MA_R:D + 2 * MA_R].rearrange("p (h e) -> p h e", e=MA_D),
                                            MA_SCALE, None, ALU.mult)
                            v.wait_ge(rot_step, done(b, 2 * NT, 2 * t + 1))
                            v.tensor_copy(g_k[t % 2][:, :, MA_D:MA_D + MA_R],
                                          new[:, 0:1, :].broadcast_to([P, MA_H, MA_R]))
                            v.tensor_scalar(g_q[t % 2][:, :, MA_D:MA_D + MA_R],
                                            new[:, 1:2, :].broadcast_to([P, MA_H, MA_R]),
                                            MA_SCALE, None, ALU.mult).then_inc(gq_ready, 1)
                            if t:
                                out_of(t - 1)
                        out_of(NT - 1)

                        def top_of(g):
                            t, h = divmod(g, MA_H)
                            v.wait_ge(gs_ready, done(b, HS, g))
                            if g >= 2:
                                v.wait_ge(gp_ready, done(b, HS, g - 2))
                            v.tensor_reduce(g_top[h % 2], bank(2 * (h % 2), 2)[:, 0:P * (t + 1)], AX.X, ALU.max,
                                            negate=True).then_inc(gtop_ready, 1)

                        def over_sums(t):
                            v.wait_ge(gsum_ready, done(b, NT, t))
                            v.reciprocal(g_over, bank(7)).then_inc(gon_step, 1)
                            v.wait_ge(gon_step, done(b, NT, t))
                            v.tensor_tensor(g_on, g_o, g_over, ALU.mult).then_inc(gon_ready, 1)

                        def add(t):
                            v.wait_ge(gwo_ready, done(b, NT, t))
                            x = x_tok[:, bass.ds(b * NT + t, 1), :].rearrange("p a d -> p (a d)")
                            v.tensor_tensor(x, bank(7)[:, 0:P], x, ALU.add).then_inc(gx_added, 1)

                        top_of(0)
                        for g in range(HS):
                            t, h = divmod(g, MA_H)
                            if g + 1 < HS:
                                top_of(g + 1)
                            for p in range(t // 4 + 1):
                                n = number[g, p]
                                if not by_a[n]:
                                    piece_out(v, v.tensor_copy, b, g, p, n).then_inc(gt_v, 1)
                            if t and h == 3:
                                over_sums(t - 1)
                            if t and h == 6:
                                add(t - 1)
                        over_sums(NT - 1)
                        add(NT - 1)

        layer_norm_tokens(True)
        layers(0)
        add_half(0)
        layer_norm_tokens(False)
        global_attention()
        layer_norm_tokens(True)
        layers(1)
        add_half(1)

        with nc.Block() as block:
            @block.sync
            def _(sp):
                sp.dma_start(out.rearrange("b (t p) d -> p (b t) d", p=P), x_tok[:]).then_inc(stored, 16)
                sp.wait_ge(stored, 16)


def window_tables():
    f = np.float32
    half = np.arange(0, DH, 2, dtype=f)
    inv = (f(1.0) / f(10000.0) ** (half / f(DH))).astype(f)
    t = np.arange(T, dtype=f)
    freqs = np.concatenate([t[:, None] * inv[None, :]] * 2, -1).astype(f)
    base = ((half + f(0.4 * DH)) / f(1.4 * DH)).astype(f)
    power = ((t - T // 2) / f(WIN // 2)).astype(f)
    scale = (base[None, :] ** power[:, None]).astype(f)
    scale = np.concatenate([scale, scale], -1)
    cos, sin = np.cos(freqs), np.sin(freqs)
    sin = np.concatenate([-sin[:, :DH // 2], sin[:, DH // 2:]], -1)
    s8 = scale * f(QK_SCALE)
    tab = np.stack([cos * s8, cos / scale, sin * s8, sin / scale], 1).astype(f)
    return np.ascontiguousarray(tab.reshape(NT, P, 4, DH).transpose(1, 0, 2, 3))


def band_mask():
    r = np.arange(P)[:, None] % WIN
    j = np.arange(2 * WIN)[None, :]
    m = np.where((j >= r) & (j <= r + WIN), 0.0, NEG)
    first = np.where((np.arange(P)[:, None] < WIN) & (j < WIN), NEG, m)
    return np.ascontiguousarray(np.stack([first] + [m] * (NT - 1), 1).reshape(P, -1).astype(np.float32))


def square_tables():
    k, m = np.arange(P)[:, None], np.arange(P)[None, :]
    sel = (k == WIN * (m // WIN) + MA_D)
    return np.ascontiguousarray(np.stack(
        [np.eye(P), sel, np.where(m > k, NEG, 0.0)], 1).astype(np.float32))


def global_rotary():
    f = np.float32
    inv = (f(1.0) / f(10000.0) ** (np.arange(0, MA_R, 2, dtype=f) / f(MA_R))).astype(f)
    a = (np.arange(T, dtype=f)[:, None] * inv[None, :]).astype(f)
    tab = np.stack([np.cos(a), np.sin(a)], 1).astype(f)
    return np.ascontiguousarray(tab.reshape(NT, P, 2, MA_R // 2).transpose(1, 0, 2, 3))


def kernel(**inputs):
    import concourse.bacc as bacc
    from concourse.bass_utils import run_bass_kernel_spmd

    g = {k: np.asarray(v) for k, v in inputs.items()}

    def pieces(a, rows):
        n = -(-rows // P)
        pad = np.zeros(a.shape[:-2] + (n * P - rows, a.shape[-1]), a.dtype)
        a = np.concatenate([a, pad], -2)
        return np.moveaxis(a.reshape(a.shape[:-2] + (n, P, a.shape[-1])), -3, -2)

    b1 = g["L0_ffn_b1"]
    cols = [pieces(b1[:, i * F:i * F + F, None], F)[..., 0] for i in range(2)]
    cols += [g[k][:, :, None] for k in ("L0_ffn_ln_g", "L0_ffn_ln_b", "L0_ffn_b2")]
    qs, ks = g["L0_ffn_q_scale"], g["L0_ffn_k_scale"]
    swap = lambda a: np.concatenate([a[:, DH // 2:], a[:, :DH // 2]], -1)
    sc = np.concatenate([qs, ks, swap(qs), swap(ks)], -1)
    ma_o = np.zeros((4, WIN, 4, D), np.float32)
    ma_o[:, :MA_D] = g["L0_attn_W_o"].reshape(4, 4, MA_D, D).transpose(1, 2, 0, 3)
    arrays = {
        "x": g["L0_attn_x"], "wqkv": g["L0_ffn_Wqkv"], "wo": pieces(g["L0_ffn_Wo"], INNER),
        "w1": g["L0_ffn_W1"], "w2": pieces(g["L0_ffn_W2"], F), "vec": np.concatenate(cols, -1),
        "scale": np.repeat(sc[:, None, :], P, 1),
        "ma_down": g["L0_attn_W_kv_down"],
        "ma_up": np.concatenate([g["L0_attn_W_k_up"], g["L0_attn_W_v_up"], g["L0_attn_W_k_rope"]], -1),
        "ma_q": np.concatenate([g["L0_attn_W_q_rope"], g["L0_attn_W_q"]], -1),
        "ma_o": ma_o.reshape(P, 4, D),
        "rotary": window_tables(), "mask": band_mask(), "square": square_tables(),
        "ma_rotary": global_rotary(),
    }
    nc = bacc.Bacc("TRN2", target_bir_lowering=False, num_devices=1)
    laid, args = {}, []
    for name, a in arrays.items():
        laid[f"in_{name}"] = np.ascontiguousarray(a)
        args.append(nc.dram_tensor(f"in_{name}", a.shape, mybir.dt.from_np(a.dtype), kind="ExternalInput").ap())
    args.append(nc.dram_tensor("out_x", (B, T, D), mybir.dt.float32, kind="ExternalOutput").ap())
    macaron_program(nc, *args)
    r = run_bass_kernel_spmd(nc, [laid], core_ids=[0])
    return r.results[0]["out_x"]
```
